# Optimizing a Trainium2 kernel written in Bass

```python
import numpy as np
import jax
import jax.numpy as jnp

def _softmax(x, axis=-1):
    return jax.nn.softmax(x, axis=axis)

def _gelu(x):
    return jax.nn.gelu(x, approximate=True)

def _silu(x):
    return jax.nn.silu(x)

def _sigmoid(x):
    return jax.nn.sigmoid(x)

def _layernorm(x, axis=-1, eps=1e-05):
    m = jnp.mean(x, axis=axis, keepdims=True)
    v = jnp.var(x, axis=axis, keepdims=True)
    return (x - m) / jnp.sqrt(v + eps)

def _scatter_add(tgt, idx, src, axis=0):
    return tgt.at[idx].add(src)

def _segment_sum(src, seg, n):
    return jax.ops.segment_sum(src, seg, n)
kernel_name = 'mk_recurrent_d1_jaxref_r8_135a6a'

def setup_inputs(seed: int=0):
    np.random.seed(seed)
    _w = jnp.asarray

    def _L0_attn_setup():
        import jax, jax.numpy as jnp
        import numpy as np
        NH = 16
        key = jax.random.key(seed)
        ks = jax.random.split(key, 5)
        B, T, D = (2, 256, 256)
        scale = 0.02
        return {'x': jax.random.normal(ks[0], (B, T, D), dtype=jnp.float32), 'Wq': jax.random.normal(ks[1], (D, D), dtype=jnp.float32) * scale, 'Wk': jax.random.normal(ks[2], (D, D), dtype=jnp.float32) * scale, 'Wv': jax.random.normal(ks[3], (D, D), dtype=jnp.float32) * scale, 'Wo': jax.random.normal(ks[4], (D, D), dtype=jnp.float32) * scale}
    _L0_attn_in = _L0_attn_setup()

    def _L0_ffn_setup():
        import jax, jax.numpy as jnp
        import numpy as np
        DIM = 256
        HID = 704
        ZERO_POINT = 128.0

        def _qlinear(x, wq, scale):
            W = (wq.astype(jnp.float32) - ZERO_POINT) * scale[:, None]
            return jnp.einsum('bsd,hd->bsh', x, W)
        key = jax.random.key(seed)
        ks = jax.random.split(key, 7)
        B, S = (4, 256)
        sg = jax.random.uniform(ks[1], (HID,)) * (0.02 / np.sqrt(DIM)) + 0.0001
        su = jax.random.uniform(ks[3], (HID,)) * (0.02 / np.sqrt(DIM)) + 0.0001
        sd = jax.random.uniform(ks[5], (DIM,)) * (0.02 / np.sqrt(HID)) + 0.0001
        return {'x': jax.random.normal(ks[0], (B, S, DIM), dtype=jnp.float32), 'wq_gate': jax.random.randint(ks[2], (HID, DIM), 0, 32, dtype=jnp.int32), 's_gate': sg, 'wq_up': jax.random.randint(ks[4], (HID, DIM), 0, 32, dtype=jnp.int32), 's_up': su, 'wq_down': jax.random.randint(ks[6], (DIM, HID), 0, 32, dtype=jnp.int32), 's_down': sd}
    _L0_ffn_in = _L0_ffn_setup()
    _d = {'L0_attn_x': _L0_attn_in['x'], 'L0_attn_Wq': _L0_attn_in['Wq'], 'L0_attn_Wk': _L0_attn_in['Wk'], 'L0_attn_Wv': _L0_attn_in['Wv'], 'L0_attn_Wo': _L0_attn_in['Wo'], 'L0_ffn_wq_gate': _L0_ffn_in['wq_gate'], 'L0_ffn_s_gate': _L0_ffn_in['s_gate'], 'L0_ffn_wq_up': _L0_ffn_in['wq_up'], 'L0_ffn_s_up': _L0_ffn_in['s_up'], 'L0_ffn_wq_down': _L0_ffn_in['wq_down'], 'L0_ffn_s_down': _L0_ffn_in['s_down']}
    _x0 = _d['L0_attn_x']
    _d['L0_attn_x'] = jax.random.normal(jax.random.fold_in(jax.random.key(seed), 1), (4, 512, 256), dtype=_x0.dtype)
    del _x0
    return _d

def reference(L0_attn_x, L0_attn_Wq, L0_attn_Wk, L0_attn_Wv, L0_attn_Wo, L0_ffn_wq_gate, L0_ffn_s_gate, L0_ffn_wq_up, L0_ffn_s_up, L0_ffn_wq_down, L0_ffn_s_down):

    def _L0_attn_ref(x, Wq, Wk, Wv, Wo):
        import jax, jax.numpy as jnp
        import numpy as np
        NH = 16
        B, T, D = x.shape
        hd = D // NH
        q = (x @ Wq.T).reshape(B, T, NH, hd).transpose(0, 2, 1, 3)
        k = (x @ Wk.T).reshape(B, T, NH, hd).transpose(0, 2, 1, 3)
        v = (x @ Wv.T).reshape(B, T, NH, hd).transpose(0, 2, 1, 3)
        att = jnp.einsum('bhtd,bhsd->bhts', q, k) / jnp.sqrt(jnp.asarray(hd, x.dtype))
        neg = jnp.finfo(att.dtype).min
        mask = jnp.triu(jnp.full((T, T), neg, dtype=att.dtype), k=1)
        att = att + mask
        w = jax.nn.softmax(att, axis=-1)
        z = jnp.einsum('bhts,bhsd->bhtd', w, v)
        z = z.transpose(0, 2, 1, 3).reshape(B, T, D)
        return z @ Wo.T

    def _L0_ffn_ref(x, wq_gate, s_gate, wq_up, s_up, wq_down, s_down):
        import jax, jax.numpy as jnp
        import numpy as np
        DIM = 256
        HID = 704
        ZERO_POINT = 128.0

        def _qlinear(x, wq, scale):
            W = (wq.astype(jnp.float32) - ZERO_POINT) * scale[:, None]
            return jnp.einsum('bsd,hd->bsh', x, W)
        gate = _qlinear(x, wq_gate, s_gate)
        gate = jax.nn.silu(gate)
        up = _qlinear(x, wq_up, s_up)
        return _qlinear(gate * up, wq_down, s_down)
    x = L0_attn_x
    xn = _layernorm(x, axis=-1)
    s = _L0_attn_ref(xn, L0_attn_Wq, L0_attn_Wk, L0_attn_Wv, L0_attn_Wo)
    g = _silu(_L0_ffn_ref(xn, L0_ffn_wq_gate, L0_ffn_s_gate, L0_ffn_wq_up, L0_ffn_s_up, L0_ffn_wq_down, L0_ffn_s_down))
    x = x + s * g
    return x

_drawn_inputs = setup_inputs


def setup_inputs(seed=0):
    import zlib

    import numpy as np

    out = dict(_drawn_inputs(seed))
    spreads = {}
    factors = {'L0_attn_Wq': 8.0,
     'L0_attn_Wk': 8.0,
     'L0_attn_Wv': 8.0,
     'L0_attn_Wo': 8.0,
     'L0_ffn_s_gate': 8.0,
     'L0_ffn_s_up': 8.0,
     'L0_ffn_s_down': 8.0}
    for name, (base, spread) in spreads.items():
        noise = np.random.default_rng([zlib.crc32(name.encode()), seed]).standard_normal(out[name].shape)
        drawn = base * np.exp(spread * noise) if base else spread * noise
        out[name] = jnp.asarray(drawn.astype(out[name].dtype))
    for name, factor in factors.items():
        out[name] = (out[name] * factor).astype(out[name].dtype)
    return out
```

```python
from contextlib import ExitStack

import concourse.bass as bass
from concourse import mybir

ALU = mybir.AluOpType
ACT = mybir.ActivationFunctionType
F32 = mybir.dt.float32
F32R = mybir.dt.float32r
BF16 = mybir.dt.bfloat16
I32 = mybir.dt.int32

P = 128
B, T, D = 4, 512, 256
NH, HD = 16, 16
HID = 704
KD = D // P
TT = T // P
HT = -(-HID // P)
HIDP = HT * P
GH = 4
NG = NH // GH
HH = NH // 2
UNITS = GH * TT
SLOTS = 10
ROWC = 3 * HD
EPS = 1e-5
ZERO_POINT = 128.0
SCALE = float(HD) ** -0.5
NEG = -1e38
LOWEST = -3e38
MAGIC = float(0x5F3759DF)
NEWTON = 4
LN_STEPS = 2 * TT + 3 + 3 * NEWTON

SM0, SM1, ST0, ST1, BZ, GA, GB, MI = range(8)


def slot_blocks(k):
    if k < GH:
        return [(k, 0, 0)]
    if k < 2 * GH:
        return [(k - GH, 1, 0), (k - GH, 3, 3 * P)]
    return [(2 * (k - 2 * GH), 2, 0), (2 * (k - 2 * GH) + 1, 2, 2 * P)]


SLOT_OF = {(a, j): (k, c) for k in range(SLOTS) for a, j, c in slot_blocks(k)}
UNITS_AFTER = [UNITS * (k + 1) // SLOTS for k in range(SLOTS)]


def build(nc, x, wqkvT, woT, wgT, wuT, wdT, sg, su, sd, out):
    with ExitStack() as ctx:
        def sb(name, shape, dt=F32):
            return ctx.enter_context(nc.sbuf_tensor(name, shape, dt))

        def sem(name):
            return ctx.enter_context(nc.semaphore(name))

        ps = ctx.enter_context(nc.psum_tensor("ps", [P, 8, 512], F32))

        qp = sb("qp", [P, NH, T], F32R)
        kp = sb("kp", [P, NH, T], F32R)
        pt = sb("pt", [P, SLOTS, T])
        vt = sb("vt", [P, TT, NH, HD + 1])
        xin = sb("xin", [P, TT, D])
        xh = sb("xh", [P, KD, T], F32R)
        xl = sb("xl", [P, KD, T], F32R)
        wh = sb("wh", [P, KD, 3 * D], F32R)
        wl = sb("wl", [P, KD, 3 * D], F32R)
        woh = sb("woh", [P, KD, D], F32R)
        wol = sb("wol", [P, KD, D], F32R)
        guh = sb("guh", [P, 2, KD, HIDP], F32R)
        gul = sb("gul", [P, 2, KD, HIDP], F32R)
        wdh = sb("wdh", [P, HT, D], F32R)
        wdl = sb("wdl", [P, HT, D], F32R)
        hh = sb("hh", [P, HT, T], F32R)
        hl = sb("hl", [P, HT, T], F32R)
        xn = sb("xn", [P, TT, D])
        zbuf = sb("zbuf", [P, 3, T])
        zs = zbuf[:, 0, :]
        zc = zbuf[:, 1, :]
        lc = zbuf[:, 2, :]
        zh = sb("zh", [P, 2, T], F32R)
        zl = sb("zl", [P, 2, T], F32R)
        act = sb("act", [P, 2, T])
        u = sb("u", [P, TT, D])
        fth = sb("fth", [P, D])
        tri = sb("tri", [P, T], BF16)
        ident = sb("ident", [P, P])
        sdb = sb("sdb", [P, D])
        cn = sb("cn", [P, P])
        cr = sb("cr", [P, UNITS], F32R)
        ctr = sb("ctr", [32, P], F32R)
        mx = sb("mx", [P, UNITS])
        stats = sb("stats", [P, TT, 6])
        mv = sb("mv", [P, TT, 2])
        nw = sb("nw", [P, 4, TT])
        nwi = sb("nwi", [P, 2, TT], I32)
        sgt = sb("sgt", [P, 3, HT])
        hsg = sb("hsg", [P, HT])
        ones = sb("ones", [P, 1])

        qk_dram = nc.dram_tensor("qk_scratch", [2, 2, 2, P, T], F32, kind="Internal").ap()
        z_dram = nc.dram_tensor("z_scratch", [NG, P, T], F32, kind="Internal").ap()
        zero_dram = nc.dram_tensor("zero_scratch", [2, HH, T], F32, kind="Internal").ap()

        x_loaded = sem("x_loaded")
        wqkv_loaded, wo_loaded, gu_loaded, wd_loaded = map(
            sem, ("wqkv_loaded", "wo_loaded", "gu_loaded", "wd_loaded"))
        sc_loaded, sd_loaded, zero_stored = map(sem, ("sc_loaded", "sd_loaded", "zero_stored"))
        qk_stored = [sem("qk_stored_a"), sem("qk_stored_b")]
        pack_loaded = [sem("pack_loaded_a"), sem("pack_loaded_b")]
        c_loaded = sem("c_loaded")
        z_stored = sem("z_stored")
        z_loaded = [sem("z_loaded_a"), sem("z_loaded_b")]
        res_loaded, out_stored = sem("res_loaded"), sem("out_stored")
        consts, pool_step, gu_float, wd_float = map(sem, ("consts", "pool_step", "gu_float", "wd_float"))
        qp_zero, kp_zero, kp_ones, row_one = map(sem, ("qp_zero", "kp_zero", "kp_ones", "row_one"))
        hi_done, lo_done, sc_step = map(sem, ("hi_done", "lo_done", "sc_step"))
        ln_step, xn_done, xt_ready, xhi_done, xlo_done = map(
            sem, ("ln_step", "xn_done", "xt_ready", "xhi_done", "xlo_done"))
        qk_ready, qhi_done, qlo_done, v_ready, v_done = map(
            sem, ("qk_ready", "qhi_done", "qlo_done", "v_ready", "v_done"))
        gu_ready, tanh_done, gate_done, h_done, hhi_done, hlo_done = map(
            sem, ("gu_ready", "tanh_done", "gate_done", "h_done", "hhi_done", "hlo_done"))
        f_ready, f_done, fth_done, u_done = map(sem, ("f_ready", "f_done", "fth_done", "u_done"))
        sm_ready, max_done, cr_done, cn_done, ct_ready, ct_copied = map(
            sem, ("sm_ready", "max_done", "cr_done", "cn_done", "ct_ready", "ct_copied"))
        st_ready, exp_done, mask_done, pv_done, z_copied = map(
            sem, ("st_ready", "exp_done", "mask_done", "pv_done", "z_copied"))
        rl_done, zn_done, zhi_done, o_ready, o_used, out_done = map(
            sem, ("rl_done", "zn_done", "zhi_done", "o_ready", "o_used", "out_done"))
        zlo_done = [sem("zlo_done_a"), sem("zlo_done_b")]

        stage = [pt[:, 2 * c:2 * c + 2, :] for c in range(4)]
        flat = pt[:].rearrange("p s n -> p (s n)")
        n_qkv, n_o, n_gu = KD * 3 * D, KD * D, 2 * KD * HIDP
        raw_qkv = flat[:, 0:n_qkv]
        raw_o = flat[:, n_qkv:n_qkv + n_o]
        raw_gu = flat[:, n_qkv + n_o:n_qkv + n_o + n_gu]
        raw_d = zbuf[:].rearrange("p a n -> p (a n)")

        def first(b):
            return isinstance(b, int) and b == 0

        def carry(engine, register):
            engine.reg_alu(register, register, 1, ALU.bitwise_or)

        block = ctx.enter_context(nc.Block())

        @block.sync
        def _(sp):
            sp.dma_start(xin[:], x[0].rearrange("(i p) d -> p i d", p=P)).then_inc(x_loaded, 16)
            sp.dma_start(raw_qkv.rearrange("p (k n) -> p k n", k=KD),
                         wqkvT.rearrange("(k p) n -> p k n", p=P)).then_inc(wqkv_loaded, 16)
            g4 = raw_gu.bitcast(I32).rearrange("p (w k n) -> p w k n", w=2, k=KD)
            sp.dma_start(g4[:, 0], wgT.rearrange("(k p) n -> p k n", p=P)).then_inc(gu_loaded, 16)
            sp.dma_start(g4[:, 1], wuT.rearrange("(k p) n -> p k n", p=P)).then_inc(gu_loaded, 16)
            sp.dma_start(raw_o.rearrange("p (k n) -> p k n", k=KD),
                         woT.rearrange("(k p) n -> p k n", p=P)).then_inc(wo_loaded, 16)
            sp.dma_start(sgt[:, 0, :], sg).then_inc(sc_loaded, 16)
            sp.dma_start(sgt[:, 1, :], su).then_inc(sc_loaded, 16)
            sp.dma_start(sdb[:], sd.rearrange("(a d) -> a d", a=1).to_broadcast([P, D])).then_inc(sd_loaded, 16)
            sp.wait_ge(qp_zero, 2)
            sp.dma_start(zero_dram, qp[64:66, 0:HH, :].bitcast(F32)).then_inc(zero_stored, 16)
            sp.dma_start(raw_d.bitcast(I32).rearrange("p (m n) -> p m n", m=HT),
                         wdT.rearrange("(m p) n -> p m n", p=P)).then_inc(wd_loaded, 16)
            sp.wait_ge(zero_stored, 16)
            sp.wait_ge(kp_ones, 1)

            def z_trip(b, g):
                half, part = g // 2, 64 * (g % 2)
                sp.wait_ge(z_copied, NG * b + g + 1)
                sp.dma_start(z_dram[g], zs).then_inc(z_stored, 16)
                sp.wait_ge(z_stored, 16 * (NG * b + g + 1))
                if g == 0 and not first(b):
                    sp.wait_ge(zlo_done[1], b)
                if g == 2:
                    sp.wait_ge(zlo_done[0], b + 1)
                rows = z_dram[g].rearrange("(a r) n -> a r n", a=GH)
                sp.dma_start(zbuf[part:part + 64, 1, :], rows[:, 0:HD, :]).then_inc(z_loaded[half], 16)
                sp.dma_start(zbuf[part:part + 64, 2, :],
                             rows[:, HD:HD + 1, :].to_broadcast([GH, HD, T])).then_inc(z_loaded[half], 16)

            def c_rows(b, g):
                sp.wait_ge(ct_copied, NG * b + g + 1)
                for r in range(2):
                    sp.dma_start(qp[ROWC + r:ROWC + r + 1, GH * g:GH * (g + 1), :].bitcast(F32).rearrange(
                        "p a (i n) -> p (a i) n", i=TT), ctr[UNITS * r:UNITS * (r + 1), :].bitcast(F32)).then_inc(c_loaded, 16)

            def store_out(b, p):
                sp.wait_ge(out_done, 2 * b + p + 1)
                sp.dma_start(out[b].rearrange("(i p) d -> p i d", p=P)[:, 2 * p:2 * p + 2, :],
                             xin[:, 2 * p:2 * p + 2, :]).then_inc(out_stored, 16)

            def stack(b, half):
                heads = slice(HH * half, HH * (half + 1))
                sp.wait_ge(qk_stored[half], 32 * (b + 1))
                for w, buf, order in ((0, qp, (0, 1, 0)), (1, kp, (0, 0, 1))):
                    for r, part in enumerate(order):
                        sp.dma_start(buf[HD * r:HD * (r + 1), heads, :].bitcast(F32),
                                     qk_dram[w, half, part].rearrange("(h d) n -> d h n", d=HD)
                                     ).then_inc(pack_loaded[half], 16)
                sp.dma_start(qp[ROWC:ROWC + 2, heads, :].bitcast(F32), zero_dram).then_inc(pack_loaded[half], 16)

            def batch(b):
                for c in range(4):
                    half, which = c // 2, c % 2
                    sp.wait_ge(qlo_done, 4 * b + c + 1)
                    sp.dma_start(qk_dram[which, half].rearrange("s p n -> p s n"), stage[c]).then_inc(qk_stored[half], 16)
                if not first(b):
                    sp.wait_ge(st_ready, NG * SLOTS * b)
                stack(b, 0)
                stack(b, 1)
                if not first(b):
                    sp.wait_ge(xn_done, TT * (b + 1))
                    sp.dma_start(xin[:], x[b - 1].rearrange("(i p) d -> p i d", p=P)).then_inc(res_loaded, 16)
                c_rows(b, 0)
                if not first(b):
                    store_out(b - 1, 0)
                    store_out(b - 1, 1)
                c_rows(b, 1)
                if first(b):
                    sp.wait_ge(xn_done, TT)
                else:
                    sp.wait_ge(out_stored, 32 * b)
                sp.dma_start(xin[:], x[b + 1].rearrange("(i p) d -> p i d", p=P)).then_inc(x_loaded, 16)
                for g in range(NG):
                    if g + 2 < NG:
                        c_rows(b, g + 2)
                    z_trip(b, g)

            batch(0)
            with sp.Fori(1, B) as b:
                batch(b)
            store_out(B - 1, 0)
            store_out(B - 1, 1)
            sp.wait_ge(out_stored, 32 * B)

        @block.tensor
        def _(pe):
            def split3(dst, lh, ll, rh, rl, start, stop):
                nc.tensor.matmul(dst, lh, rh, start=start, stop=False)
                nc.tensor.matmul(dst, lh, rl, start=False, stop=False)
                return nc.tensor.matmul(dst, ll, rh, start=False, stop=stop)

            def transpose_x(b):
                for k in range(KD):
                    bank = GA + k
                    if k == 0:
                        pe.wait_ge(xn_done, TT * (b + 1))
                        if not first(b):
                            pe.wait_ge(h_done, HT * b)
                    for i in range(TT):
                        last = nc.tensor.transpose(ps[:, bank, i * P:(i + 1) * P],
                                                   xn[:, i, k * P:(k + 1) * P], ident[:])
                    last.then_inc(xt_ready, 1)

            def project_qk(b):
                pe.wait_ge(xlo_done, KD * (b + 1))
                if first(b):
                    pe.wait_ge(hi_done, 1)
                    pe.wait_ge(lo_done, 1)
                for c, bank in enumerate((MI, SM0, SM1, MI)):
                    half, which = c // 2, c % 2
                    if c == 0 and not first(b):
                        pe.wait_ge(f_done, TT * b)
                    if c == 1 and not first(b):
                        pe.wait_ge(ct_copied, NG * b)
                    if c == 3:
                        pe.wait_ge(qlo_done, 4 * b + 1)
                    col = which * D + half * P
                    for k in range(KD):
                        last = split3(ps[:, bank, :], wh[:, k, col:col + P], wl[:, k, col:col + P],
                                      xh[:, k, :], xl[:, k, :], k == 0, k == KD - 1)
                    last.then_inc(qk_ready, 1)

            def project_v(b):
                for n in range(2):
                    if n == 0 and not first(b):
                        pe.wait_ge(exp_done, 4 * SLOTS * b)
                    for i in (2 * n, 2 * n + 1):
                        for k in range(KD):
                            rows = slice(i * P, (i + 1) * P)
                            dst = ps[:, ST0 + n, (i % 2) * D:(i % 2 + 1) * D]
                            last = split3(dst, xh[:, k, rows], xl[:, k, rows], wh[:, k, 2 * D:], wl[:, k, 2 * D:],
                                          k == 0, k == KD - 1)
                    last.then_inc(v_ready, 1)

            def gate_up(b, m, between=None):
                banks = (GA, GB) if m % 2 == 0 else (MI, BZ)
                if m == 0 and first(b):
                    pe.wait_ge(hi_done, 4)
                    pe.wait_ge(lo_done, 4)
                if m == 1:
                    pe.wait_ge(qlo_done, 4 * b + 4)
                    if not first(b):
                        pe.wait_ge(z_copied, NG * b)
                if m >= 2:
                    pe.wait_ge(h_done, HT * b + m - 1)
                cols = slice(m * P, (m + 1) * P)
                for w in range(2):
                    for k in range(KD):
                        last = split3(ps[:, banks[w], :], guh[:, w, k, cols], gul[:, w, k, cols],
                                      xh[:, k, :], xl[:, k, :], k == 0, k == KD - 1)
                        if between and (w, k) != (1, 1):
                            between(2 * w + k)
                last.then_inc(gu_ready, 1)
                if between:
                    between(3)

            def maxima_unit(b, g, n):
                a, i = n // TT, n % TT
                h = GH * g + a
                if n == 0:
                    if g % 2 == 0:
                        pe.wait_ge(pack_loaded[g // 2], 16 * 7 * (b + 1))
                    if g == 0:
                        pe.wait_ge(qlo_done, 4 * b + 3)
                    else:
                        pe.wait_ge(ct_copied, NG * b + g)
                    if g == 1 and not first(b):
                        pe.wait_ge(o_used, 2 * b)
                if n >= 2:
                    pe.wait_ge(max_done, NG * UNITS * b + UNITS * g + n - 1)
                w = (i + 1) * P
                nc.tensor.matmul(ps[:, SM0 + n % 2, 0:w], qp[:, h, i * P:(i + 1) * P], kp[:, h, 0:w],
                                 start=True, stop=True).then_inc(sm_ready, 1)

            def transpose_c(b, g):
                pe.wait_ge(cn_done, 2 * (NG * b + g + 1))
                nc.tensor.transpose(ps[:, SM0, 0:P], cn[:], ident[:]).then_inc(ct_ready, 1)

            def project_out(b):
                for half in range(2):
                    pe.wait_ge(zlo_done[half], b + 1)
                pe.wait_ge(ct_copied, NG * (b + 1) + 1)
                out_tiles()

            def out_tiles():
                for n in range(2):
                    for i in (2 * n, 2 * n + 1):
                        rows = slice(i * P, (i + 1) * P)
                        for k in range(2):
                            dst = ps[:, SM0 + n, (i % 2) * D:(i % 2 + 1) * D]
                            last = split3(dst, zh[:, k, rows], zl[:, k, rows], woh[:, k, :], wol[:, k, :],
                                          k == 0, k == 1)
                    last.then_inc(o_ready, 1)

            def scores_slot(b, g, k):
                if k == 0:
                    pe.wait_ge(c_loaded, 32 * (NG * b + g + 1))
                n = SLOTS * g + k
                if n < 2:
                    pe.wait_ge(v_done, 2 * b + n + 1)
                else:
                    pe.wait_ge(exp_done, NG * SLOTS * b + n - 1)
                blocks = slot_blocks(k)
                for a, j, c in blocks:
                    h = GH * g + a
                    last = nc.tensor.matmul(ps[:, ST0 + n % 2, c:c + T - j * P], kp[:, h, j * P:(j + 1) * P],
                                            qp[:, h, j * P:], start=True, stop=True)
                last.then_inc(st_ready, 1)

            def values(b, g, js, stage):
                if js[0] == 0 and g == 0:
                    pe.wait_ge(h_done, HT * (b + 1))
                elif js[0] == 0:
                    pe.wait_ge(z_copied, NG * b + g)
                pe.wait_ge(mask_done, SLOTS * (NG * b + g) + (4, 8, 10)[stage])
                for j in js:
                    for a in range(GH):
                        k, c = SLOT_OF[a, j]
                        last = nc.tensor.matmul(ps[32 * a:32 * a + HD + 1, BZ, j * P:],
                                                vt[:, j, GH * g + a, :], pt[:, k, c:c + T - j * P],
                                                start=(j == 0), stop=(j == 2))
                last.then_inc(pv_done, 1)

            def project_down(b, i):
                if i == 0:
                    pe.wait_ge(hlo_done, HT * (b + 1))
                    if first(b):
                        pe.wait_ge(hi_done, 5)
                        pe.wait_ge(lo_done, 5)
                else:
                    pe.wait_ge(f_done, TT * b + i)
                rows = slice(i * P, (i + 1) * P)
                for m in range(HT):
                    last = split3(ps[:, MI, 0:D], hh[:, m, rows], hl[:, m, rows], wdh[:, m, :], wdl[:, m, :],
                                  m == 0, m == HT - 1)
                last.then_inc(f_ready, 1)

            def batch(b):
                transpose_x(b)
                project_qk(b)
                gate_up(b, 0)
                project_v(b)
                gate_up(b, 1)
                for m in (2, 3):
                    gate_up(b, m, lambda q: [maxima_unit(b, 0, 8 * (m - 2) + 2 * q + r) for r in range(2)])
                transpose_c(b, 0)
                if not first(b):
                    project_out(b - 1)
                for m in (4, 5):
                    gate_up(b, m, lambda q: [maxima_unit(b, 1, 8 * (m - 4) + 2 * q + r) for r in range(2)])
                transpose_c(b, 1)
                for g in range(NG):
                    for k in range(SLOTS):
                        scores_slot(b, g, k)
                        if g + 2 < NG:
                            for n in range(UNITS_AFTER[k - 1] if k else 0, UNITS_AFTER[k]):
                                maxima_unit(b, g + 2, n)
                        if k == 8:
                            values(b, g, (0,), 0)
                    if g + 2 < NG:
                        transpose_c(b, g + 2)
                    values(b, g, (1, 3), 1)
                    project_down(b, g)
                    values(b, g, (2,), 2)

            pe.wait_ge(consts, 2)
            batch(0)
            with pe.Fori(1, B) as b:
                batch(b)
            for half in range(2):
                pe.wait_ge(zlo_done[half], B)
            out_tiles()

        @block.scalar
        def _(act_e):
            act_e.wait_ge(wqkv_loaded, 16)
            nc.scalar.copy(wh[:].rearrange("p k n -> p (k n)"), raw_qkv).then_inc(hi_done, 1)
            act_e.wait_ge(wo_loaded, 16)
            nc.scalar.copy(woh[:].rearrange("p k n -> p (k n)"), raw_o).then_inc(hi_done, 1)

            def split_gu_hi():
                for w in range(2):
                    act_e.wait_ge(gu_float, w + 1)
                    nc.scalar.copy(guh[:, w].rearrange("p k n -> p (k n)"),
                                   raw_gu[:, w * KD * HIDP:(w + 1) * KD * HIDP]).then_inc(hi_done, 1)

            def batch(b):
                for k in range(KD):
                    act_e.wait_ge(xt_ready, KD * b + k + 1)
                    if k == 0 and not first(b):
                        act_e.wait_ge(v_ready, 2 * b)
                        act_e.wait_ge(gu_ready, HT * b)
                    nc.scalar.copy(xh[:, k, :], ps[:, GA + k, :]).then_inc(xhi_done, 1)
                for c, bank in enumerate((MI, SM0, SM1, MI)):
                    act_e.wait_ge(qk_ready, 4 * b + c + 1)
                    if c == 0 and not first(b):
                        act_e.wait_ge(pv_done, 3 * NG * b)
                    if first(b) and c == 2:
                        split_gu_hi()
                    if first(b):
                        act_e.wait_ge(lo_done, 2 if c < 2 else 4)
                    nc.scalar.copy(stage[c][:, 0, :].bitcast(F32R), ps[:, bank, :]).then_inc(qhi_done, 1)
                for m in range(HT):
                    if m == 1:
                        for n in range(2):
                            act_e.wait_ge(v_ready, 2 * b + n + 1)
                            if n == 0 and not first(b):
                                act_e.wait_ge(pv_done, 3 * NG * b)
                            nc.scalar.copy(vt[:, 2 * n:2 * n + 2, :, 0:HD],
                                           ps[:, ST0 + n, :].rearrange("p (i h d) -> p i h d", i=2, d=HD)
                                           ).then_inc(v_done, 1)
                    act_e.wait_ge(gu_ready, HT * b + m + 1)
                    if m >= 2 or not first(b):
                        act_e.wait_ge(hlo_done, HT * b + m - 1)
                    if m == 0 and first(b):
                        act_e.wait_ge(sc_step, 1)
                    gbank = GA if m % 2 == 0 else MI
                    nc.scalar.activation(act[:, m % 2, :], ps[:, gbank, :], ACT.Tanh,
                                         scale=hsg[:, m:m + 1]).then_inc(tanh_done, 1)
                if first(b):
                    act_e.wait_ge(wd_float, 1)
                    nc.scalar.copy(wdh[:].rearrange("p m n -> p (m n)"), raw_d).then_inc(hi_done, 1)
                    act_e.wait_ge(lo_done, 5)
                for g in range(NG):
                    for k in range(SLOTS):
                        act_e.wait_ge(st_ready, SLOTS * (NG * b + g) + k + 1)
                        if k in (0, 4, 8) and not (first(b) and g == 0):
                            act_e.wait_ge(pv_done, 3 * (NG * b + g) - 2 + k // 4)
                        nc.scalar.activation(pt[:, k, :], ps[:, ST0 + k % 2, :], ACT.Exp,
                                             scale=SCALE).then_inc(exp_done, 1)
                    act_e.wait_ge(f_done, TT * b + g + 1)
                    if g or not first(b):
                        act_e.wait_ge(u_done, TT * b + g)
                    nc.scalar.activation(fth[:], u[:, g, :], ACT.Tanh, scale=0.5).then_inc(fth_done, 1)
                    act_e.wait_ge(pv_done, 3 * (NG * b + g + 1))
                    if g or not first(b):
                        act_e.wait_ge(z_stored, 16 * (NG * b + g))
                    nc.scalar.copy(zs, ps[:, BZ, :]).then_inc(z_copied, 1)

            batch(0)
            with act_e.Fori(1, B) as b:
                batch(b)

        @block.gpsimd
        def _(pool):
            spare = pool.alloc_register("pool_spare")
            pool.reg_mov(spare, 1)
            nc.gpsimd.memset(ident[:], 0.0).then_inc(pool_step, 1)
            nc.gpsimd.memset(tri[:], 0.0).then_inc(pool_step, 1)
            nc.gpsimd.memset(ones[:], 1.0).then_inc(pool_step, 1)
            pool.wait_ge(pool_step, 3)
            nc.gpsimd.affine_select(out=ident[:], in_=ident[:], compare_op=ALU.not_equal, fill=1.0, base=0,
                                    pattern=[[-1, P]], channel_multiplier=1).then_inc(consts, 1)
            nc.gpsimd.affine_select(out=tri[:, T - P:], in_=tri[:, T - P:], compare_op=ALU.is_ge, fill=NEG,
                                    base=0, pattern=[[-1, P]], channel_multiplier=1).then_inc(consts, 1)
            nc.gpsimd.affine_select(out=ones[:], in_=ones[:], compare_op=ALU.is_ge, fill=0.0,
                                    base=-ROWC, pattern=[[0, 1]], channel_multiplier=1).then_inc(pool_step, 1)
            pool.wait_ge(pool_step, 4)
            nc.gpsimd.affine_select(out=ones[:], in_=ones[:], compare_op=ALU.is_ge, fill=0.0,
                                    base=ROWC + 1, pattern=[[0, 1]], channel_multiplier=-1).then_inc(row_one, 1)
            for w in range(2):
                pool.wait_ge(gu_loaded, 32)
                part = raw_gu[:, w * KD * HIDP:(w + 1) * KD * HIDP]
                nc.gpsimd.tensor_scalar(part, part.bitcast(I32), -ZERO_POINT, 1.0, ALU.add, ALU.mult).then_inc(gu_float, 1)
            pool.wait_ge(gu_float, 2)
            nc.gpsimd.memset(qp[32:64].bitcast(F32), 0.0).then_inc(qp_zero, 1)
            nc.gpsimd.memset(qp[64:P].bitcast(F32), 0.0).then_inc(qp_zero, 1)

            pool.wait_ge(qp_zero, 2)

            def split_z(b, half):
                n = 2 * b + half
                pool.wait_ge(zn_done, n + 1)
                if half == 0 and not first(b):
                    pool.wait_ge(o_ready, 2 * b)
                carry(pool, spare)
                nc.gpsimd.tensor_scalar(zh[:, half, :], zc, 1.0, 1.0, ALU.mult, ALU.mult).then_inc(zhi_done, 1)
                pool.wait_ge(zhi_done, n + 1)
                nc.gpsimd.tensor_tensor(zl[:, half, :], zc, zh[:, half, :].bitcast(F32),
                                        ALU.subtract).then_inc(zlo_done[half], 1)

            def batch(b):
                for m in range(HT):
                    if m == 2 and not first(b):
                        split_z(b - 1, 1)
                    pool.wait_ge(h_done, HT * b + m + 1)
                    if m == 0 and not first(b):
                        pool.wait_ge(f_ready, TT * b)
                    carry(pool, spare)
                    nc.gpsimd.tensor_scalar(hh[:, m, :], act[:, m % 2, :], 1.0, 1.0, ALU.mult, ALU.mult).then_inc(hhi_done, 1)
                    pool.wait_ge(hhi_done, HT * b + m + 1)
                    nc.gpsimd.tensor_tensor(hl[:, m, :], act[:, m % 2, :], hh[:, m, :].bitcast(F32),
                                            ALU.subtract).then_inc(hlo_done, 1)
                if first(b):
                    pool.wait_ge(wd_loaded, 16)
                    nc.gpsimd.tensor_scalar(raw_d, raw_d.bitcast(I32), -ZERO_POINT, 1.0, ALU.add, ALU.mult).then_inc(wd_float, 1)
                for g in range(NG):
                    for k in range(SLOTS):
                        pool.wait_ge(exp_done, SLOTS * (NG * b + g) + k + 1)
                        blocks = pt[:, k, :].rearrange("p (a c) -> p a c", c=P)
                        step = (4, 3, 2)[k // GH]
                        diag = blocks[:, 0:4:step, :] if k >= GH else blocks[:, 0:1, :]
                        carry(pool, spare)
                        nc.gpsimd.affine_select(out=diag, in_=diag, compare_op=ALU.is_ge, fill=0.0, base=0,
                                                pattern=[[0, diag.shape[1]], [1, P]],
                                                channel_multiplier=-1).then_inc(mask_done, 1)
                    if g == 3:
                        split_z(b, 0)

            batch(0)
            with pool.Fori(1, B) as b:
                batch(b)
            split_z(B - 1, 1)
            pool.wait_ge(consts, spare)

        @block.vector
        def _(dve):
            spare = dve.alloc_register("dve_spare")
            dve.reg_mov(spare, 1)
            nc.vector.memset(kp[64:P].bitcast(F32), 0.0).then_inc(kp_zero, 1)
            nc.vector.memset(vt[:, :, :, HD:HD + 1], 1.0).then_inc(kp_zero, 1)
            nc.vector.memset(cn[:], 0.0).then_inc(kp_zero, 1)
            nc.vector.memset(pt_zero_view(kp)[:], 0.0).then_inc(kp_zero, 1)

            def newton(b):
                s = [LN_STEPS * b]

                def step(ins, wait=True):
                    s[0] = s[0] + 1
                    ins.then_inc(ln_step, 1)
                    if wait:
                        dve.wait_ge(ln_step, s[0])

                dve.wait_ge(x_loaded, 16 * (b + 1))
                if not first(b):
                    dve.wait_ge(xt_ready, KD * b)
                for i in range(TT):
                    step(nc.vector.bn_stats(stats[:, i, :], xin[:, i, :]), i == TT - 1)
                carry(dve, spare)
                for i in range(TT):
                    step(nc.vector.bn_aggr(mv[:, i, :], stats[:, i, :]), i == TT - 1)
                v, y, t = nw[:, 0, :], nw[:, 1, :], nw[:, 2, :]
                step(nc.vector.tensor_scalar(v, mv[:, :, 1], EPS, None, ALU.add))
                step(nc.vector.tensor_scalar(nwi[:, 0, :], v.bitcast(I32), 1, None, ALU.logical_shift_right))
                step(nc.vector.tensor_scalar(y.bitcast(I32), nwi[:, 0, :], -1.0, MAGIC, ALU.mult, ALU.add))
                for _ in range(NEWTON):
                    step(nc.vector.tensor_tensor(t, y, y, ALU.mult))
                    step(nc.vector.scalar_tensor_tensor(t, t, -0.5, v, ALU.mult, ALU.mult))
                    step(nc.vector.scalar_tensor_tensor(y, t, 1.5, y, ALU.add, ALU.mult))
                for i in range(TT):
                    nc.vector.tensor_scalar(xn[:, i, :], xin[:, i, :], mv[:, i, 0:1], nw[:, 1, i:i + 1],
                                            ALU.subtract, ALU.mult).then_inc(xn_done, 1)

            def split_gu_lo():
                for w in range(2):
                    dve.wait_ge(hi_done, 3 + w)
                    nc.vector.tensor_tensor(gul[:, w].rearrange("p k n -> p (k n)"),
                                            raw_gu[:, w * KD * HIDP:(w + 1) * KD * HIDP],
                                            guh[:, w].rearrange("p k n -> p (k n)").bitcast(F32),
                                            ALU.subtract).then_inc(lo_done, 1)

            def norm_z(b, half):
                n = 2 * b + half
                dve.wait_ge(z_loaded[half], 64 * (b + 1))
                nc.vector.reciprocal(lc, lc).then_inc(rl_done, 1)
                dve.wait_ge(rl_done, n + 1)
                nc.vector.tensor_tensor(zc, zc, lc, ALU.mult).then_inc(zn_done, 1)

            def hidden(b, m):
                gbank, ubank = (GA, GB) if m % 2 == 0 else (MI, BZ)
                a = act[:, m % 2, :]
                n = HT * b + m + 1
                dve.wait_ge(tanh_done, n)
                nc.vector.scalar_tensor_tensor(a, a, 1.0, ps[:, gbank, :], ALU.add, ALU.mult).then_inc(gate_done, 1)
                dve.wait_ge(gate_done, n)
                nc.vector.scalar_tensor_tensor(a, ps[:, ubank, :], sgt[:, 2, m:m + 1], a,
                                               ALU.mult, ALU.mult).then_inc(h_done, 1)

            def maxima(b, g, n):
                i = n % TT
                w = (i + 1) * P
                s = ps[:, SM0 + n % 2, 0:w]
                dve.wait_ge(sm_ready, UNITS * (NG * b + g) + n + 1)
                if n == 0 and (g or not first(b)):
                    dve.wait_ge(cn_done, 2 * (NG * b + g))
                carry(dve, spare)
                nc.vector.tensor_tensor_reduce(s, s, tri[:, T - w:], 1.0, LOWEST, ALU.add, ALU.max,
                                               mx[:, n:n + 1]).then_inc(max_done, 1)

            def negate(b, g):
                n = NG * b + g + 1
                dve.wait_ge(max_done, UNITS * n)
                if g or not first(b):
                    dve.wait_ge(ct_ready, n - 1)
                nc.vector.tensor_scalar(cr[:], mx[:], -1.0, None, ALU.mult).then_inc(cr_done, 1)
                dve.wait_ge(cr_done, n)
                nc.vector.tensor_copy(cn[:, 0:UNITS], cr[:].bitcast(F32)).then_inc(cn_done, 1)
                nc.vector.scalar_tensor_tensor(cn[:, UNITS:2 * UNITS], mx[:], -1.0, cr[:].bitcast(F32),
                                               ALU.mult, ALU.subtract).then_inc(cn_done, 1)
                dve.wait_ge(ct_ready, n)
                if g or not first(b):
                    dve.wait_ge(c_loaded, 32 * (n - 1))
                nc.vector.tensor_copy(ctr[:], ps[0:32, SM0, 0:P]).then_inc(ct_copied, 1)

            def finish(b):
                for n in range(2):
                    k = 2 * b + n + 1
                    dve.wait_ge(o_ready, k)
                    un = u[:, 2 * n:2 * n + 2, :]
                    nc.vector.scalar_tensor_tensor(un, ps[:, SM0 + n, :].rearrange("p (i d) -> p i d", i=2), 0.5, un,
                                                   ALU.mult, ALU.mult).then_inc(o_used, 1)
                    dve.wait_ge(o_used, k)
                    yield_wait(b, n)
                    nc.vector.tensor_tensor(xin[:, 2 * n:2 * n + 2, :], xin[:, 2 * n:2 * n + 2, :], un,
                                            ALU.add).then_inc(out_done, 1)

            def yield_wait(b, n):
                if n == 0:
                    if isinstance(b, int) and b == B - 1:
                        dve.wait_ge(x_loaded, 16 * (B + 1))
                    else:
                        dve.wait_ge(res_loaded, 16 * (b + 1))

            def ffn_out(b, i):
                n = TT * b + i + 1
                dve.wait_ge(f_ready, n)
                if i == 0:
                    if first(b):
                        dve.wait_ge(sd_loaded, 16)
                    else:
                        dve.wait_ge(out_done, 2 * b)
                nc.vector.tensor_tensor(u[:, i, :], ps[:, MI, 0:D], sdb[:], ALU.mult).then_inc(f_done, 1)
                dve.wait_ge(fth_done, n)
                nc.vector.scalar_tensor_tensor(u[:, i, :], fth[:], 1.0, u[:, i, :],
                                               ALU.add, ALU.mult).then_inc(u_done, 1)

            def batch(b):
                for k in range(KD):
                    dve.wait_ge(xhi_done, KD * b + k + 1)
                    nc.vector.tensor_tensor(xl[:, k, :], ps[:, GA + k, :], xh[:, k, :].bitcast(F32),
                                            ALU.subtract).then_inc(xlo_done, 1)
                for c, bank in enumerate((MI, SM0, SM1, MI)):
                    if first(b) and c == 2:
                        split_gu_lo()
                    dve.wait_ge(qhi_done, 4 * b + c + 1)
                    nc.vector.tensor_tensor(stage[c][:, 1, :].bitcast(F32R), ps[:, bank, :], stage[c][:, 0, :],
                                            ALU.subtract).then_inc(qlo_done, 1)
                if first(b):
                    dve.wait_ge(sc_loaded, 32)
                    nc.vector.tensor_scalar(hsg[:], sgt[:, 0, :], 0.5, None, ALU.mult).then_inc(sc_step, 1)
                    dve.wait_ge(sc_step, 1)
                    nc.vector.tensor_tensor(sgt[:, 2, :], hsg[:], sgt[:, 1, :], ALU.mult).then_inc(sc_step, 1)
                    dve.wait_ge(sc_step, 2)
                hidden(b, 0)
                hidden(b, 1)
                if not first(b):
                    norm_z(b - 1, 1)
                for g in (0, 1):
                    for r in range(2):
                        for n in range(8 * r, 8 * r + 8):
                            maxima(b, g, n)
                        hidden(b, 2 + 2 * g + r)
                    negate(b, g)
                    if g == 0 and not first(b):
                        finish(b - 1)
                if first(b):
                    dve.wait_ge(hi_done, 5)
                    nc.vector.tensor_tensor(wdl[:].rearrange("p m n -> p (m n)"), raw_d,
                                            wdh[:].rearrange("p m n -> p (m n)").bitcast(F32),
                                            ALU.subtract).then_inc(lo_done, 1)
                for g in range(NG):
                    if g + 2 < NG:
                        for n in range(UNITS):
                            maxima(b, g + 2, n)
                        negate(b, g + 2)
                    if g == 3:
                        norm_z(b, 0)
                    ffn_out(b, g)
                    if g == 2:
                        newton(b + 1)

            dve.wait_ge(hi_done, 1)
            nc.vector.tensor_tensor(wl[:].rearrange("p k n -> p (k n)"), raw_qkv,
                                    wh[:].rearrange("p k n -> p (k n)").bitcast(F32),
                                    ALU.subtract).then_inc(lo_done, 1)
            dve.wait_ge(hi_done, 2)
            nc.vector.tensor_tensor(wol[:].rearrange("p k n -> p (k n)"), raw_o,
                                    woh[:].rearrange("p k n -> p (k n)").bitcast(F32),
                                    ALU.subtract).then_inc(lo_done, 1)
            dve.wait_ge(row_one, 1)
            dve.wait_ge(kp_zero, 4)
            rows = kp[32:64].rearrange("p h n -> p (h n)")
            nc.vector.tensor_scalar(rows, rows.bitcast(F32), ones[32:64, :], None, ALU.add).then_inc(kp_ones, 1)
            newton(0)
            batch(0)
            with dve.Fori(1, B) as b:
                batch(b)
            dve.wait_ge(consts, spare)
            norm_z(B - 1, 1)
            finish(B - 1)


def pt_zero_view(kp):
    return kp[32:64].bitcast(F32)


def kernel(**inputs):
    import numpy as np
    import concourse.bacc as bacc
    from concourse.bass_utils import run_bass_kernel_spmd as run

    a = {k.replace("L0_", ""): np.asarray(v) for k, v in inputs.items()}
    pad = HIDP - HID
    arrays = {
        "x": np.ascontiguousarray(np.concatenate([a["attn_x"], a["attn_x"][B - 1:]])),
        "wqkvT": np.ascontiguousarray(np.concatenate([a["attn_Wq"], a["attn_Wk"], a["attn_Wv"]]).T),
        "woT": np.ascontiguousarray(a["attn_Wo"].T),
        "wgT": np.pad(a["ffn_wq_gate"].T, ((0, 0), (0, pad))),
        "wuT": np.pad(a["ffn_wq_up"].T, ((0, 0), (0, pad))),
        "wdT": np.pad(a["ffn_wq_down"].T, ((0, pad), (0, 0))),
        "sg": np.ascontiguousarray(np.pad(a["ffn_s_gate"], (0, pad)).reshape(HT, P).T),
        "su": np.ascontiguousarray(np.pad(a["ffn_s_up"], (0, pad)).reshape(HT, P).T),
        "sd": a["ffn_s_down"],
    }
    nc = bacc.Bacc("TRN2", target_bir_lowering=False, num_devices=1)
    aps = [nc.dram_tensor(f"in_{n}", v.shape, mybir.dt.from_np(v.dtype), kind="ExternalInput").ap()
           for n, v in arrays.items()]
    out = nc.dram_tensor("out_0", (B, T, D), F32, kind="ExternalOutput").ap()
    build(nc, *aps, out)
    r = run(nc, [{f"in_{n}": v for n, v in arrays.items()}], core_ids=[0])
    return r.results[0]["out_0"]
```

```python
from contextlib import ExitStack

import concourse.bass as bass
from concourse import mybir

ALU = mybir.AluOpType
ACT = mybir.ActivationFunctionType
F32 = mybir.dt.float32
F32R = mybir.dt.float32r
BF16 = mybir.dt.bfloat16
I32 = mybir.dt.int32

P = 128
B, T, D = 4, 512, 256
NH, HD = 16, 16
HID = 704
KD = D // P
TT = T // P
HT = -(-HID // P)
HIDP = HT * P
GH = 4
NG = NH // GH
HH = NH // 2
UNITS = GH * TT
SLOTS = 10
RC = T // HD
Z_TILE = 3
ROWC = 3 * HD
EPS = 1e-5
ZERO_POINT = 128.0
SCALE = float(HD) ** -0.5
NEG = -1e38
LOWEST = -3e38
MAGIC = float(0x5F3759DF)
NEWTON = 3
LN_STEPS = TT + 3 + 3 * NEWTON

SM0, SM1, ST0, ST1, BZ, GA, GB, MI = range(8)
MAX_RING = ((SM0, SM1, ST0, ST1), (SM0, SM1, GA))
ST_RING = (GB, ST0, ST1)
QK_BANKS = (GA, SM0, GA, SM1)
QK_SLOTS = (1, 3, 5, 7)

TILE_SLOTS = {m: [divmod(4 * (m - 1) + q, SLOTS) for q in range(4)] for m in range(1, HT)}


def max_bank(g, k):
    ring = MAX_RING[g // 2]
    return ring[(SLOTS * g + k) % 4] if g < 2 else ring[k % 3]


def slot_blocks(k):
    if k < GH:
        return [(k, 0, 0)]
    if k < 2 * GH:
        return [(k - GH, 1, 0), (k - GH, 3, 3 * P)]
    return [(2 * (k - 2 * GH), 2, 0), (2 * (k - 2 * GH) + 1, 2, 2 * P)]


SLOT_OF = {(a, j): (k, c) for k in range(SLOTS) for a, j, c in slot_blocks(k)}


def max_blocks(k):
    return [(a, TT - 1 - j, c) for a, j, c in slot_blocks(k)]


def build(nc, x, wqkvT, woT, wgT, wuT, wdT, sg, su, sd, out):
    with ExitStack() as ctx:
        def sb(name, shape, dt=F32):
            return ctx.enter_context(nc.sbuf_tensor(name, shape, dt))

        def sem(name):
            return ctx.enter_context(nc.semaphore(name))

        ps = ctx.enter_context(nc.psum_tensor("ps", [P, 8, 512], F32))

        qp = sb("qp", [P, NH, T], F32R)
        kp = sb("kp", [P, NH, T], F32R)
        pt = sb("pt", [P, SLOTS, T])
        vt = sb("vt", [P, TT, NH, HD + 1])
        xin = sb("xin", [P, TT, D])
        xh = sb("xh", [P, KD, T], F32R)
        xl = sb("xl", [P, KD, T], F32R)
        wh = sb("wh", [P, KD, 3 * D], F32R)
        wl = sb("wl", [P, KD, 3 * D], F32R)
        woh = sb("woh", [P, KD, D], F32R)
        wol = sb("wol", [P, KD, D], F32R)
        guh = sb("guh", [P, 2, KD, HIDP], F32R)
        gul = sb("gul", [P, 2, KD, HIDP], F32R)
        wdh = sb("wdh", [P, HT, D], F32R)
        wdl = sb("wdl", [P, HT, D], F32R)
        hh = sb("hh", [P, HT, T], F32R)
        hl = sb("hl", [P, HT, T], F32R)
        xn = sb("xn", [P, TT, D])
        zbuf = sb("zbuf", [P, 3, T])
        zs = zbuf[:, 0, :]
        zc = zbuf[:, 1, :]
        lc = zbuf[:, 2, :]
        rl = sb("rl", [P, RC])
        zh = sb("zh", [P, 2, T], F32R)
        zl = sb("zl", [P, 2, T], F32R)
        act = sb("act", [P, 2, T])
        u = sb("u", [P, TT, D])
        fth = sb("fth", [P, D])
        tri = sb("tri", [P, T], BF16)
        ident = sb("ident", [P, P])
        sdb = sb("sdb", [P, D])
        cn = sb("cn", [P, P])
        ctr = sb("ctr", [32, P], F32R)
        mx = sb("mx", [P, UNITS])
        stats = sb("stats", [P, TT, 6])
        mv = sb("mv", [P, TT, 2])
        nw = sb("nw", [P, 4, TT])
        nwi = sb("nwi", [P, 2, TT], I32)
        sgt = sb("sgt", [P, 3, HT])
        hsg = sb("hsg", [P, HT])

        qk_dram = nc.dram_tensor("qk_scratch", [2, 2, HH, 2, HD, T], F32, kind="Internal").ap()
        z_dram = nc.dram_tensor("z_scratch", [NG, P, T], F32, kind="Internal").ap()
        rl_dram = nc.dram_tensor("rl_scratch", [2, HH, T], F32, kind="Internal").ap()
        zero_dram = nc.dram_tensor("zero_scratch", [2, HH, T], F32, kind="Internal").ap()

        x_loaded = sem("x_loaded")
        wqkv_loaded, wo_loaded, gu_loaded, wd_loaded = map(
            sem, ("wqkv_loaded", "wo_loaded", "gu_loaded", "wd_loaded"))
        sc_loaded, sd_loaded, zero_stored = map(sem, ("sc_loaded", "sd_loaded", "zero_stored"))
        qk_stored = [sem(f"qk_stored_{c}") for c in range(4)]
        pack_loaded = [sem("pack_loaded_a"), sem("pack_loaded_b")]
        c_loaded = sem("c_loaded")
        z_stored = sem("z_stored")
        l_loaded = [sem("l_loaded_a"), sem("l_loaded_b")]
        rl_stored = sem("rl_stored")
        z_loaded = [sem("z_loaded_a"), sem("z_loaded_b")]
        res_loaded, out_stored = sem("res_loaded"), sem("out_stored")
        consts, pool_step, gu_float, wd_float = map(sem, ("consts", "pool_step", "gu_float", "wd_float"))
        qp_zero, kp_zero, dve_const = map(sem, ("qp_zero", "kp_zero", "dve_const"))
        kp_ones = [sem("kp_ones_a"), sem("kp_ones_b")]
        hi_done, lo_done, sc_step = map(sem, ("hi_done", "lo_done", "sc_step"))
        stats_done, ln_step, xn_done, xt_ready, xhi_done, xlo_done = map(
            sem, ("stats_done", "ln_step", "xn_done", "xt_ready", "xhi_done", "xlo_done"))
        qk_ready, qhi_done, qlo_done, v_ready, v_done = map(
            sem, ("qk_ready", "qhi_done", "qlo_done", "v_ready", "v_done"))
        gu_ready, tanh_done, gate_done, h_done, hhi_done, hlo_done = map(
            sem, ("gu_ready", "tanh_done", "gate_done", "h_done", "hhi_done", "hlo_done"))
        f_ready, f_done, fth_done, u_done = map(sem, ("f_ready", "f_done", "fth_done", "u_done"))
        sm_ready, max_done, cn_done, ct_ready, ct_copied = map(
            sem, ("sm_ready", "max_done", "cn_done", "ct_ready", "ct_copied"))
        st_ready, exp_done, mask_done, pv_done, z_copied = map(
            sem, ("st_ready", "exp_done", "mask_done", "pv_done", "z_copied"))
        rl_done, zn_done, zhi_done, o_ready, o_used, out_done = map(
            sem, ("rl_done", "zn_done", "zhi_done", "o_ready", "o_used", "out_done"))
        zlo_done = [sem("zlo_done_a"), sem("zlo_done_b")]

        stage = [act[:], xn[:].rearrange("p i d -> p (i d)").rearrange("p (s n) -> p s n", s=2),
                 hl[:, HT - 2:, :].bitcast(F32), hh[:, HT - 2:, :].bitcast(F32)]
        flat = pt[:].rearrange("p s n -> p (s n)")
        n_qkv, n_o, n_gu = KD * 3 * D, KD * D, 2 * KD * HIDP
        raw_qkv = flat[:, 0:n_qkv]
        raw_o = flat[:, n_qkv:n_qkv + n_o]
        raw_gu = flat[:, n_qkv + n_o:n_qkv + n_o + n_gu]
        raw_d = zbuf[:].rearrange("p a n -> p (a n)")

        def first(b):
            return isinstance(b, int) and b == 0

        def last(b):
            return isinstance(b, int) and b == B - 1

        def carry(engine, register):
            engine.reg_alu(register, register, 1, ALU.bitwise_or)

        block = ctx.enter_context(nc.Block())

        @block.sync
        def _(sp):
            sp.dma_start(xin[:], x[0].rearrange("(i p) d -> p i d", p=P)).then_inc(x_loaded, 16)
            sp.dma_start(raw_qkv.rearrange("p (k n) -> p k n", k=KD),
                         wqkvT.rearrange("(k p) n -> p k n", p=P)).then_inc(wqkv_loaded, 16)
            g4 = raw_gu.bitcast(I32).rearrange("p (w k n) -> p w k n", w=2, k=KD)
            sp.dma_start(g4[:, 0], wgT.rearrange("(k p) n -> p k n", p=P)).then_inc(gu_loaded, 16)
            sp.dma_start(g4[:, 1], wuT.rearrange("(k p) n -> p k n", p=P)).then_inc(gu_loaded, 16)
            sp.dma_start(raw_o.rearrange("p (k n) -> p k n", k=KD),
                         woT.rearrange("(k p) n -> p k n", p=P)).then_inc(wo_loaded, 16)
            sp.dma_start(sgt[:, 0, :], sg).then_inc(sc_loaded, 16)
            sp.dma_start(sgt[:, 1, :], su).then_inc(sc_loaded, 16)
            sp.dma_start(sdb[:], sd.rearrange("(a d) -> a d", a=1).to_broadcast([P, D])).then_inc(sd_loaded, 16)
            sp.dma_start(raw_d.bitcast(I32).rearrange("p (m n) -> p m n", m=HT),
                         wdT.rearrange("(m p) n -> p m n", p=P)).then_inc(wd_loaded, 16)
            sp.wait_ge(qp_zero, 1)
            sp.dma_start(zero_dram, qp[64:66, 0:HH, :].bitcast(F32)).then_inc(zero_stored, 16)
            sp.wait_ge(dve_const, 1)
            sp.wait_ge(zero_stored, 16)

            def k_ones(half):
                sp.wait_ge(qp_zero, half + 1)
                sp.wait_ge(kp_zero, half + 1)
                sp.dma_start(kp[ROWC:ROWC + 2, HH * half:HH * (half + 1), :].bitcast(F32),
                             u[0:HH, :, :]).then_inc(kp_ones[half], 16)

            def store_z(b, g):
                sp.wait_ge(z_copied, NG * b + g + 1)
                load_sums(b, g)
                sp.dma_start(z_dram[g], zs).then_inc(z_stored, 16)

            def z_in_scratch(b, g):
                sp.wait_ge(z_stored, 16 * (NG * b + g + 1))

            def load_z(b, g):
                half, part = g // 2, 64 * (g % 2)
                if g == 0 and not first(b):
                    sp.wait_ge(zlo_done[1], b)
                if g == 2:
                    sp.wait_ge(zlo_done[0], b + 1)
                rows = z_dram[g].rearrange("(a r) n -> a r n", a=GH)
                sp.dma_start(zbuf[part:part + 64, 1, :], rows[:, 0:HD, :]).then_inc(z_loaded[half], 16)

            def load_sums(b, g):
                half, part = g // 2, 64 * (g % 2)
                if g == 2:
                    sp.wait_ge(rl_stored, 16 * (2 * b + 1))
                elif g == 0 and not first(b):
                    sp.wait_ge(rl_stored, 32 * b)
                sp.dma_start(rl[part:part + 64, :], zbuf[HD::32, 0, :]).then_inc(l_loaded[half], 16)

            def rl_trip(b, half):
                sp.wait_ge(rl_done, 2 * b + half + 1)
                sp.dma_start(rl_dram[half], rl[:]).then_inc(rl_stored, 16)
                sp.wait_ge(rl_stored, 16 * (2 * b + half + 1))
                sp.dma_start(lc, rl_dram[half].rearrange("h (o n) -> h o n", o=1).to_broadcast([HH, HD, T])
                             ).then_inc(z_loaded[half], 16)

            def c_rows(b, g):
                sp.wait_ge(ct_copied, NG * b + g + 1)
                sp.dma_start(qp[ROWC:ROWC + 2, GH * g:GH * (g + 1), :].bitcast(F32),
                             ctr[:].bitcast(F32)).then_inc(c_loaded, 16)

            def store_out(b, p):
                sp.wait_ge(out_done, 2 * b + p + 1)
                sp.dma_start(out[b].rearrange("(i p) d -> p i d", p=P)[:, 2 * p:2 * p + 2, :],
                             xin[:, 2 * p:2 * p + 2, :]).then_inc(out_stored, 16)

            def stack(b, half, ws=(0, 1)):
                heads = slice(HH * half, HH * (half + 1))
                if first(b) and 0 in ws:
                    k_ones(half)
                for w in ws:
                    buf, both, again = ((qp, 0, 2 * HD), (kp, HD, 0))[w]
                    sp.wait_ge(qk_stored[2 * half + w], 32 * (b + 1))
                    sp.dma_start(buf[both:both + 2 * HD, heads, :].bitcast(F32),
                                 qk_dram[w, half].rearrange("h s d n -> (s d) h n")).then_inc(pack_loaded[half], 16)
                    sp.dma_start(buf[again:again + HD, heads, :].bitcast(F32),
                                 qk_dram[w, half, :, 0].rearrange("h d n -> d h n")).then_inc(pack_loaded[half], 16)
                    if w == 0:
                        sp.dma_start(qp[ROWC:ROWC + 2, heads, :].bitcast(F32), zero_dram).then_inc(pack_loaded[half], 16)

            def batch(b):
                if not first(b):
                    store_z(b - 1, 3)
                    z_in_scratch(b - 1, 3)
                    load_z(b - 1, 2)
                    load_z(b - 1, 3)
                    rl_trip(b - 1, 1)
                stack(b, 1)
                c_rows(b, 0)
                if first(b):
                    sp.wait_ge(xn_done, TT)
                else:
                    store_out(b - 1, 0)
                    store_out(b - 1, 1)
                    sp.wait_ge(out_stored, 32 * b)
                sp.dma_start(xin[:], x[B - 1 if last(b) else b + 1].rearrange("(i p) d -> p i d", p=P)
                             ).then_inc(x_loaded, 16)
                c_rows(b, 1)
                c_rows(b, 2)
                store_z(b, 0)
                z_in_scratch(b, 0)
                load_z(b, 0)
                c_rows(b, 3)
                store_z(b, 1)
                z_in_scratch(b, 1)
                load_z(b, 1)
                if not last(b):
                    sp.wait_ge(xn_done, TT * (b + 2))
                    sp.dma_start(xin[:], x[b].rearrange("(i p) d -> p i d", p=P)).then_inc(res_loaded, 16)
                rl_trip(b, 0)
                if not last(b):
                    stack(b + 1, 0, (0,))
                store_z(b, 2)
                if not last(b):
                    stack(b + 1, 0, (1,))

            stack(0, 0)
            batch(0)
            with sp.Fori(1, B - 1) as b:
                batch(b)
            batch(B - 1)
            store_z(B - 1, 3)
            z_in_scratch(B - 1, 3)
            load_z(B - 1, 2)
            load_z(B - 1, 3)
            rl_trip(B - 1, 1)
            store_out(B - 1, 0)
            store_out(B - 1, 1)
            sp.wait_ge(out_stored, 32 * B)

        @block.tensor
        def _(pe):
            def split3(dst, lh, ll, rh, rl, start, stop):
                nc.tensor.matmul(dst, lh, rh, start=start, stop=False)
                nc.tensor.matmul(dst, lh, rl, start=False, stop=False)
                return nc.tensor.matmul(dst, ll, rh, start=False, stop=stop)

            def transpose_x(b):
                pe.wait_ge(xn_done, TT * (b + 1))
                if not first(b):
                    pe.wait_ge(max_done, NG * SLOTS * b)
                for k in range(KD):
                    for i in range(TT):
                        last = nc.tensor.transpose(ps[:, SM0 + k, i * P:(i + 1) * P],
                                                   xn[:, i, k * P:(k + 1) * P], ident[:])
                    last.then_inc(xt_ready, 1)

            def project_qk(b, c):
                if c == 0:
                    pe.wait_ge(xlo_done, KD * (b + 1))
                    if first(b):
                        pe.wait_ge(hi_done, 1)
                        pe.wait_ge(lo_done, 1)
                if c == 2:
                    pe.wait_ge(qlo_done, 4 * b + 1)
                col = (c % 2) * D + (c // 2) * P
                for k in range(KD):
                    mm = split3(ps[:, QK_BANKS[c], :], wh[:, k, col:col + P], wl[:, k, col:col + P],
                                xh[:, k, :], xl[:, k, :], k == 0, k == KD - 1)
                mm.then_inc(qk_ready, 1)

            def project_v(b):
                for n in range(2):
                    for i in (2 * n, 2 * n + 1):
                        for k in range(KD):
                            rows = slice(i * P, (i + 1) * P)
                            dst = ps[:, ST0 + n, (i % 2) * D:(i % 2 + 1) * D]
                            last = split3(dst, xh[:, k, rows], xl[:, k, rows], wh[:, k, 2 * D:], wl[:, k, 2 * D:],
                                          k == 0, k == KD - 1)
                    last.then_inc(v_ready, 1)

            def gate_up(b, m, between=None):
                banks = (GA, GB) if m % 2 == 0 else (MI, BZ)
                if m == 0:
                    pe.wait_ge(qlo_done, 4 * b + 3)
                if m == 1 and not first(b):
                    pe.wait_ge(f_done, TT * b)
                if m >= 2:
                    pe.wait_ge(h_done, HT * b + m - 1)
                cols = slice(m * P, (m + 1) * P)
                for w in range(2):
                    if m == 0 and first(b):
                        pe.wait_ge(hi_done, 2 + w)
                        pe.wait_ge(lo_done, 2 + w)
                    if w == 1 and m == 0 and not first(b):
                        pe.wait_ge(exp_done, NG * SLOTS * b)
                    if w == 1 and m == 1 and not first(b):
                        pe.wait_ge(z_copied, NG * b)
                    if w == 1 and m == HT - 1:
                        pe.wait_ge(ct_copied, NG * b + 1)
                    for k in range(KD):
                        last = split3(ps[:, banks[w], :], guh[:, w, k, cols], gul[:, w, k, cols],
                                      xh[:, k, :], xl[:, k, :], k == 0, k == KD - 1)
                        if between and (w, k) != (1, 1):
                            between(2 * w + k)
                last.then_inc(gu_ready, 1)
                if between:
                    between(3)

            def maxima_slot(b, g, k):
                if k == 0 and g % 2 == 0:
                    pe.wait_ge(pack_loaded[g // 2], 16 * 5 * (b + 1))
                if k == 0 and first(b) and g % 2 == 0:
                    pe.wait_ge(kp_ones[g // 2], 16)
                n = SLOTS * g + k
                if g == 0 and k == 1:
                    pe.wait_ge(qlo_done, 4 * b + 4)
                if g == 0 and k == 2:
                    pe.wait_ge(v_done, 2 * b + 2)
                if g == 1 and k in (6, 7) and not first(b):
                    pe.wait_ge(o_used, 2 * (b - 1) + k - 5)
                if g == 2 and k == 2:
                    pe.wait_ge(h_done, HT * b + 5)
                depth = len(MAX_RING[g // 2])
                if g < 2 and n >= depth:
                    pe.wait_ge(max_done, NG * SLOTS * b + n - depth + 1)
                if g >= 2 and (g, k) != (2, 2):
                    before = {0: (g - 1, 6 if g == 2 else 9), 1: (g - 1, 7 if g == 2 else 7), 2: (g - 1, 8)}
                    pg, pk = before[k] if k < depth else (g, k - depth)
                    pe.wait_ge(max_done, NG * SLOTS * b + SLOTS * pg + pk + 1)
                for a, i, c in max_blocks(k):
                    h, w = GH * g + a, (i + 1) * P
                    last = nc.tensor.matmul(ps[:, max_bank(g, k), c:c + w], qp[:, h, i * P:(i + 1) * P],
                                            kp[:, h, 0:w], start=True, stop=True)
                last.then_inc(sm_ready, 1)

            def transpose_c(b, g):
                pe.wait_ge(cn_done, 2 * (NG * b + g + 1))
                if g < 2:
                    pe.wait_ge(h_done, HT * b + (4 if g == 0 else HT))
                else:
                    pe.wait_ge(f_done, TT * b + g - 1)
                dst = ps[:, BZ, 0:P] if g == 0 else ps[:, MI, 0:P]
                nc.tensor.transpose(dst, cn[:], ident[:]).then_inc(ct_ready, 1)

            def project_out(b, over_maxima=True):
                for half in range(2):
                    pe.wait_ge(zlo_done[half], b + 1)
                if over_maxima:
                    pe.wait_ge(max_done, NG * SLOTS * (b + 1) + 14)
                for n in range(2):
                    for i in (2 * n, 2 * n + 1):
                        rows = slice(i * P, (i + 1) * P)
                        for k in range(2):
                            dst = ps[:, SM0 + n, (i % 2) * D:(i % 2 + 1) * D]
                            mm = split3(dst, zh[:, k, rows], zl[:, k, rows], woh[:, k, :], wol[:, k, :],
                                        k == 0, k == 1)
                    mm.then_inc(o_ready, 1)

            def scores_slot(b, g, k):
                if k == 0:
                    pe.wait_ge(c_loaded, 16 * (NG * b + g + 1))
                n = SLOTS * g + k
                if n == 0:
                    pe.wait_ge(h_done, HT * b + 5)
                elif n < 3:
                    pe.wait_ge(max_done, NG * SLOTS * b + 2 * SLOTS - 2 + n)
                else:
                    pe.wait_ge(exp_done, NG * SLOTS * b + n - 2)
                blocks = slot_blocks(k)
                for a, j, c in blocks:
                    h = GH * g + a
                    last = nc.tensor.matmul(ps[:, ST_RING[n % 3], c:c + T - j * P], kp[:, h, j * P:(j + 1) * P],
                                            qp[:, h, j * P:], start=True, stop=True)
                last.then_inc(st_ready, 1)

            def values(b, g, js, stage):
                if js[0] == 0 and g == 0:
                    pe.wait_ge(h_done, HT * (b + 1))
                elif js[0] == 0:
                    pe.wait_ge(z_copied, NG * b + g)
                pe.wait_ge(mask_done, SLOTS * (NG * b + g) + (4, 8, 10)[stage])
                for j in js:
                    for a in range(GH):
                        k, c = SLOT_OF[a, j]
                        last = nc.tensor.matmul(ps[32 * a:32 * a + HD + 1, BZ, j * P:],
                                                vt[:, j, GH * g + a, :], pt[:, k, c:c + T - j * P],
                                                start=(j == 0), stop=(j == 2))
                last.then_inc(pv_done, 1)

            def project_down(b, i, ms):
                if ms[0] == 0 and i == 0:
                    pe.wait_ge(hlo_done, HT * (b + 1))
                    if first(b):
                        pe.wait_ge(hi_done, 5)
                        pe.wait_ge(lo_done, 5)
                elif ms[0] == 0:
                    pe.wait_ge(f_done, TT * b + i)
                if ms[0] == 0 and i + 1 < NG:
                    pe.wait_ge(ct_copied, NG * b + i + 2)
                rows = slice(i * P, (i + 1) * P)
                for m in ms:
                    mm = split3(ps[:, MI, 0:D], hh[:, m, rows], hl[:, m, rows], wdh[:, m, :], wdl[:, m, :],
                                m == 0, m == HT - 1)
                if ms[-1] == HT - 1:
                    mm.then_inc(f_ready, 1)

            def batch(b):
                def last_values(q):
                    if q == 0:
                        values(b - 1, 3, (1, 3), 1)
                    if q == 1:
                        values(b - 1, 3, (2,), 2)

                gate_up(b, 0, None if first(b) else last_values)
                project_v(b)
                for m in range(1, HT):
                    gate_up(b, m, lambda q: maxima_slot(b, *TILE_SLOTS[m][q]))
                    if m == HT - 2:
                        if not first(b):
                            project_out(b - 1)
                        transpose_c(b, 0)
                for g in range(NG):
                    for k in range(SLOTS):
                        scores_slot(b, g, k)
                        if g + 2 < NG:
                            maxima_slot(b, g + 2, k)
                        if g and k == 1:
                            values(b, g - 1, (1, 3), 1)
                        if k == 2 and g + 1 < NG:
                            transpose_c(b, g + 1)
                        if g < 3 and k >= 4:
                            project_down(b, g, (k - 4,))
                        if g == 3 and k < 3:
                            project_down(b, g, (2 * k, 2 * k + 1))
                        if g and k == 4:
                            values(b, g - 1, (2,), 2)
                        if not last(b) and g == 3 and k in QK_SLOTS:
                            project_qk(b + 1, QK_SLOTS.index(k))
                        if g == 2 and k == 8 and not last(b):
                            transpose_x(b + 1)
                    values(b, g, (0,), 0)

            pe.wait_ge(consts, 2)
            transpose_x(0)
            for c in range(4):
                project_qk(0, c)
            batch(0)
            with pe.Fori(1, B - 1) as b:
                batch(b)
            batch(B - 1)
            values(B - 1, 3, (1, 3), 1)
            values(B - 1, 3, (2,), 2)
            project_out(B - 1, over_maxima=False)

        @block.scalar
        def _(act_e):
            act_e.wait_ge(wqkv_loaded, 16)
            nc.scalar.copy(wh[:].rearrange("p k n -> p (k n)"), raw_qkv).then_inc(hi_done, 1)
            def split_gu_hi(w):
                act_e.wait_ge(gu_float, w + 1)
                nc.scalar.copy(guh[:, w].rearrange("p k n -> p (k n)"),
                               raw_gu[:, w * KD * HIDP:(w + 1) * KD * HIDP]).then_inc(hi_done, 1)

            def split_x(b):
                for k in range(KD):
                    act_e.wait_ge(xt_ready, KD * b + k + 1)
                    if k == 0 and not first(b):
                        act_e.wait_ge(v_ready, 2 * b)
                        act_e.wait_ge(gu_ready, HT * b)
                    nc.scalar.copy(xh[:, k, :], ps[:, SM0 + k, :]).then_inc(xhi_done, 1)

            def chunk_hi(b, c):
                act_e.wait_ge(qk_ready, 4 * b + c + 1)
                if c < 2 and not first(b):
                    act_e.wait_ge(pack_loaded[0], 80 * b)
                    act_e.wait_ge(pack_loaded[1], 80 * b)
                if c == 0 and not first(b):
                    act_e.wait_ge(hlo_done, HT * b)
                if c == 1:
                    act_e.wait_ge(xt_ready, KD * (b + 1))
                if c == 2 and not first(b):
                    act_e.wait_ge(f_ready, TT * b)
                nc.scalar.copy(stage[c][:, 0, :].bitcast(F32R), ps[:, QK_BANKS[c], :]).then_inc(qhi_done, 1)

            def store_qk(b, c):
                act_e.wait_ge(qlo_done, 4 * b + c + 1)
                for s in range(2):
                    act_e.dma_start(qk_dram[c % 2, c // 2, :, s], stage[c][:, s, :]).then_inc(qk_stored[c], 16)

            def hidden_hi(b, m):
                act_e.wait_ge(h_done, HT * b + m + 1)
                if m == 0 and not first(b):
                    act_e.wait_ge(f_ready, TT * b)
                if m == HT - 2:
                    act_e.wait_ge(qk_stored[2], 32 * (b + 1))
                    act_e.wait_ge(qk_stored[3], 32 * (b + 1))
                nc.scalar.copy(hh[:, m, :], act[:, m % 2, :]).then_inc(hhi_done, 1)

            def z_hi(b, half):
                act_e.wait_ge(zn_done, 2 * b + half + 1)
                if half == 0 and not first(b):
                    act_e.wait_ge(o_ready, 2 * b)
                nc.scalar.copy(zh[:, half, :], zc).then_inc(zhi_done, 1)

            def copy_c(b, g):
                n = NG * b + g + 1
                act_e.wait_ge(ct_ready, n)
                if g or not first(b):
                    act_e.wait_ge(c_loaded, 16 * (n - 1))
                src = ps[0:32, BZ, 0:P] if g == 0 else ps[0:32, MI, 0:P]
                nc.scalar.copy(ctr[:], src).then_inc(ct_copied, 1)

            def copy_z(b, g):
                act_e.wait_ge(pv_done, 3 * (NG * b + g + 1))
                if g or not first(b):
                    act_e.wait_ge(z_stored, 16 * (NG * b + g))
                    act_e.wait_ge(l_loaded[(g - 1) % 4 // 2], 32 * b + 16 * ((g - 1) % 2 + 1) if g else 32 * b)
                nc.scalar.copy(zs, ps[:, BZ, :]).then_inc(z_copied, 1)

            def ffn_tanh(b, i):
                act_e.wait_ge(f_done, TT * b + i + 1)
                if i or not first(b):
                    act_e.wait_ge(u_done, TT * b + i)
                nc.scalar.activation(fth[:], u[:, i, :], ACT.Tanh, scale=0.5).then_inc(fth_done, 1)

            def batch(b):
                if not first(b):
                    ffn_tanh(b - 1, TT - 1)
                    copy_z(b - 1, NG - 1)
                for m in range(HT):
                    if m == HT - 1:
                        copy_c(b, 0)
                    act_e.wait_ge(gu_ready, HT * b + m + 1)
                    if m >= 2:
                        act_e.wait_ge(hlo_done, HT * b + m - 1)
                    if m == 0:
                        act_e.wait_ge(qk_stored[0], 32 * (b + 1))
                    if m == 0 and first(b):
                        act_e.wait_ge(sc_step, 1)
                    gbank = GA if m % 2 == 0 else MI
                    nc.scalar.activation(act[:, m % 2, :], ps[:, gbank, :], ACT.Tanh,
                                         scale=hsg[:, m:m + 1]).then_inc(tanh_done, 1)
                    if m == 0:
                        for n in range(2):
                            act_e.wait_ge(v_ready, 2 * b + n + 1)
                            nc.scalar.copy(vt[:, 2 * n:2 * n + 2, :, 0:HD],
                                           ps[:, ST0 + n, :].rearrange("p (i h d) -> p i h d", i=2, d=HD)
                                           ).then_inc(v_done, 1)
                    hidden_hi(b, m)
                    if m == Z_TILE - 1 and not first(b):
                        z_hi(b - 1, 1)
                    if m == 2 and first(b):
                        act_e.wait_ge(wd_float, 1)
                        nc.scalar.copy(wdh[:].rearrange("p m n -> p (m n)"), raw_d).then_inc(hi_done, 1)
                if first(b):
                    act_e.wait_ge(lo_done, 5)
                for g in range(NG):
                    if g == 3 and not last(b):
                        split_x(b + 1)
                    for k in range(SLOTS):
                        act_e.wait_ge(st_ready, SLOTS * (NG * b + g) + k + 1)
                        if k in (0, 4, 8) and not (first(b) and g == 0):
                            act_e.wait_ge(pv_done, 3 * (NG * b + g) - 2 + k // 4)
                        nc.scalar.activation(pt[:, k, :], ps[:, ST_RING[(SLOTS * g + k) % 3], :], ACT.Exp,
                                             scale=SCALE).then_inc(exp_done, 1)
                        if k == 1 and g:
                            ffn_tanh(b, g - 1)
                        if k == 2 and g + 1 < NG:
                            copy_c(b, g + 1)
                        if k == 6 and g:
                            copy_z(b, g - 1)
                        if g == 3 and not last(b):
                            if k - 1 in QK_SLOTS:
                                chunk_hi(b + 1, QK_SLOTS.index(k - 1))
                            if k - 2 in QK_SLOTS:
                                store_qk(b + 1, QK_SLOTS.index(k - 2))
                z_hi(b, 0)

            split_x(0)
            for c in range(4):
                if c < 2:
                    split_gu_hi(c)
                chunk_hi(0, c)
                if c:
                    store_qk(0, c - 1)
            act_e.wait_ge(wo_loaded, 16)
            nc.scalar.copy(woh[:].rearrange("p k n -> p (k n)"), raw_o).then_inc(hi_done, 1)
            store_qk(0, 3)
            batch(0)
            with act_e.Fori(1, B - 1) as b:
                batch(b)
            batch(B - 1)
            ffn_tanh(B - 1, TT - 1)
            copy_z(B - 1, NG - 1)
            z_hi(B - 1, 1)

        @block.gpsimd
        def _(pool):
            spare = pool.alloc_register("pool_spare")
            pool.reg_mov(spare, 1)
            nc.gpsimd.memset(ident[:], 0.0).then_inc(pool_step, 1)
            nc.gpsimd.memset(tri[:], 0.0).then_inc(pool_step, 1)
            pool.wait_ge(pool_step, 2)
            nc.gpsimd.affine_select(out=ident[:], in_=ident[:], compare_op=ALU.not_equal, fill=1.0, base=0,
                                    pattern=[[-1, P]], channel_multiplier=1).then_inc(consts, 1)
            nc.gpsimd.affine_select(out=tri[:, T - P:], in_=tri[:, T - P:], compare_op=ALU.is_ge, fill=NEG,
                                    base=0, pattern=[[-1, P]], channel_multiplier=1).then_inc(consts, 1)
            pool.wait_ge(consts, 2)
            for half in range(2):
                heads = slice(HH * half, HH * (half + 1))
                nc.gpsimd.memset(qp[:, heads, :].bitcast(F32), 0.0).then_inc(qp_zero, 1)
                nc.gpsimd.memset(kp[:, heads, :].bitcast(F32), 0.0).then_inc(kp_zero, 1)
                if half == 0:
                    for w in range(2):
                        pool.wait_ge(gu_loaded, 32)
                        part = raw_gu[:, w * KD * HIDP:(w + 1) * KD * HIDP]
                        nc.gpsimd.tensor_scalar(part, part.bitcast(I32), -ZERO_POINT, 1.0,
                                                ALU.add, ALU.mult).then_inc(gu_float, 1)
            pool.wait_ge(qp_zero, 2)
            pool.wait_ge(kp_zero, 2)
            pool.wait_ge(gu_float, 2)
            pool.wait_ge(wd_loaded, 16)
            nc.gpsimd.tensor_scalar(raw_d, raw_d.bitcast(I32), -ZERO_POINT, 1.0, ALU.add, ALU.mult).then_inc(wd_float, 1)

            def split_z(b, half):
                n = 2 * b + half
                pool.wait_ge(zhi_done, n + 1)
                nc.gpsimd.tensor_tensor(zl[:, half, :], zc, zh[:, half, :].bitcast(F32),
                                        ALU.subtract).then_inc(zlo_done[half], 1)

            def residual(b):
                for n in range(2):
                    if n == 0 and last(b):
                        pool.wait_ge(x_loaded, 16 * (B + 1))
                    elif n == 0:
                        pool.wait_ge(res_loaded, 16 * (b + 1))
                    pool.wait_ge(o_used, 2 * b + n + 1)
                    part = xin[:, 2 * n:2 * n + 2, :]
                    nc.gpsimd.tensor_tensor(part, part, u[:, 2 * n:2 * n + 2, :], ALU.add).then_inc(out_done, 1)

            def batch(b):
                for m in range(HT):
                    if m == Z_TILE and not first(b):
                        split_z(b - 1, 1)
                    pool.wait_ge(hhi_done, HT * b + m + 1)
                    nc.gpsimd.tensor_tensor(hl[:, m, :], act[:, m % 2, :], hh[:, m, :].bitcast(F32),
                                            ALU.subtract).then_inc(hlo_done, 1)
                    if m == 4 and not first(b):
                        residual(b - 1)
                for g in range(NG):
                    for k in range(SLOTS):
                        pool.wait_ge(exp_done, SLOTS * (NG * b + g) + k + 1)
                        blocks = pt[:, k, :].rearrange("p (a c) -> p a c", c=P)
                        step = (4, 3, 2)[k // GH]
                        diag = blocks[:, 0:4:step, :] if k >= GH else blocks[:, 0:1, :]
                        carry(pool, spare)
                        nc.gpsimd.affine_select(out=diag, in_=diag, compare_op=ALU.is_ge, fill=0.0, base=0,
                                                pattern=[[0, diag.shape[1]], [1, P]],
                                                channel_multiplier=-1).then_inc(mask_done, 1)
                split_z(b, 0)

            batch(0)
            with pool.Fori(1, B - 1) as b:
                batch(b)
            batch(B - 1)
            split_z(B - 1, 1)
            residual(B - 1)
            pool.wait_ge(consts, spare)

        @block.vector
        def _(dve):
            spare = dve.alloc_register("dve_spare")
            dve.reg_mov(spare, 1)
            nc.vector.memset(u[0:HD, :, :], 1.0).then_inc(dve_const, 1)
            nc.vector.memset(vt[:, :, :, HD:HD + 1], 1.0).then_inc(dve_const, 1)
            nc.vector.memset(cn[:], 0.0).then_inc(dve_const, 1)

            def statistics(b, i):
                if i == 0:
                    dve.wait_ge(x_loaded, 16 * (b + 1))
                nc.vector.bn_stats(stats[:, i, :], xin[:, i, :]).then_inc(stats_done, 1)

            def newton(b):
                s = [LN_STEPS * b]

                def step(ins, wait=True):
                    s[0] = s[0] + 1
                    ins.then_inc(ln_step, 1)
                    if wait:
                        dve.wait_ge(ln_step, s[0])

                dve.wait_ge(stats_done, TT * (b + 1))
                carry(dve, spare)
                for i in range(TT):
                    step(nc.vector.bn_aggr(mv[:, i, :], stats[:, i, :]), i == TT - 1)
                v, y, t = nw[:, 0, :], nw[:, 1, :], nw[:, 2, :]
                step(nc.vector.tensor_scalar(v, mv[:, :, 1], EPS, None, ALU.add))
                step(nc.vector.tensor_scalar(nwi[:, 0, :], v.bitcast(I32), 1, None, ALU.logical_shift_right))
                step(nc.vector.tensor_scalar(y.bitcast(I32), nwi[:, 0, :], -1.0, MAGIC, ALU.mult, ALU.add))
                for _ in range(NEWTON):
                    step(nc.vector.tensor_tensor(t, y, y, ALU.mult))
                    step(nc.vector.scalar_tensor_tensor(t, t, -0.5, v, ALU.mult, ALU.mult))
                    step(nc.vector.scalar_tensor_tensor(y, t, 1.5, y, ALU.add, ALU.mult))
                if not first(b):
                    dve.wait_ge(qk_stored[1], 32 * b)
                for i in range(TT):
                    nc.vector.tensor_scalar(xn[:, i, :], xin[:, i, :], mv[:, i, 0:1], nw[:, 1, i:i + 1],
                                            ALU.subtract, ALU.mult).then_inc(xn_done, 1)

            def split_gu_lo(w):
                dve.wait_ge(hi_done, 2 + w)
                nc.vector.tensor_tensor(gul[:, w].rearrange("p k n -> p (k n)"),
                                        raw_gu[:, w * KD * HIDP:(w + 1) * KD * HIDP],
                                        guh[:, w].rearrange("p k n -> p (k n)").bitcast(F32),
                                        ALU.subtract).then_inc(lo_done, 1)

            def invert_sums(b, half):
                if half or not first(b):
                    dve.wait_ge(zn_done, 2 * b + half)
                dve.wait_ge(l_loaded[half], 32 * (b + 1))
                nc.vector.reciprocal(rl[:], rl[:]).then_inc(rl_done, 1)

            def norm_z(b, half):
                dve.wait_ge(z_loaded[half], 48 * (b + 1))
                nc.vector.tensor_tensor(zc, zc, lc, ALU.mult).then_inc(zn_done, 1)

            def hidden(b, m):
                gbank, ubank = (GA, GB) if m % 2 == 0 else (MI, BZ)
                a = act[:, m % 2, :]
                n = HT * b + m + 1
                dve.wait_ge(tanh_done, n)
                nc.vector.scalar_tensor_tensor(a, a, 1.0, ps[:, gbank, :], ALU.add, ALU.mult).then_inc(gate_done, 1)
                dve.wait_ge(gate_done, n)
                nc.vector.scalar_tensor_tensor(a, ps[:, ubank, :], sgt[:, 2, m:m + 1], a,
                                               ALU.mult, ALU.mult).then_inc(h_done, 1)

            def maxima(b, g, k):
                dve.wait_ge(sm_ready, SLOTS * (NG * b + g) + k + 1)
                if k == 0 and (g or not first(b)):
                    dve.wait_ge(cn_done, 2 * (NG * b + g))
                carry(dve, spare)
                for a, i, c in max_blocks(k):
                    w = (i + 1) * P
                    s = ps[:, max_bank(g, k), c:c + w]
                    n = TT * a + i
                    last = nc.vector.tensor_tensor_reduce(s, s, tri[:, T - w:], 1.0, LOWEST, ALU.add, ALU.max,
                                                          mx[:, n:n + 1])
                last.then_inc(max_done, 1)

            def negate(b, g):
                n = NG * b + g + 1
                dve.wait_ge(max_done, SLOTS * n)
                if g or not first(b):
                    dve.wait_ge(ct_ready, n - 1)
                nc.vector.tensor_scalar(cn[:, 0:UNITS].bitcast(F32R), mx[:], -1.0, None, ALU.mult).then_inc(cn_done, 1)
                dve.wait_ge(cn_done, 2 * n - 1)
                nc.vector.scalar_tensor_tensor(cn[:, UNITS:2 * UNITS], mx[:], -1.0, cn[:, 0:UNITS],
                                               ALU.mult, ALU.subtract).then_inc(cn_done, 1)

            def finish(b):
                for n in range(2):
                    k = 2 * b + n + 1
                    dve.wait_ge(o_ready, k)
                    un = u[:, 2 * n:2 * n + 2, :]
                    nc.vector.scalar_tensor_tensor(un, ps[:, SM0 + n, :].rearrange("p (i d) -> p i d", i=2), 0.5, un,
                                                   ALU.mult, ALU.mult).then_inc(o_used, 1)

            def scale_f(b, i):
                dve.wait_ge(f_ready, TT * b + i + 1)
                if i == 0:
                    if first(b):
                        dve.wait_ge(sd_loaded, 16)
                        dve.wait_ge(kp_ones[0], 16)
                        dve.wait_ge(kp_ones[1], 16)
                    else:
                        dve.wait_ge(out_done, 2 * b)
                nc.vector.tensor_tensor(u[:, i, :], ps[:, MI, 0:D], sdb[:], ALU.mult).then_inc(f_done, 1)

            def gate_f(b, i):
                dve.wait_ge(fth_done, TT * b + i + 1)
                nc.vector.scalar_tensor_tensor(u[:, i, :], fth[:], 1.0, u[:, i, :],
                                               ALU.add, ALU.mult).then_inc(u_done, 1)

            def split_x(b):
                for k in range(KD):
                    dve.wait_ge(xhi_done, KD * b + k + 1)
                    nc.vector.tensor_tensor(xl[:, k, :], ps[:, SM0 + k, :], xh[:, k, :].bitcast(F32),
                                            ALU.subtract).then_inc(xlo_done, 1)

            def chunk_lo(b, c):
                dve.wait_ge(qhi_done, 4 * b + c + 1)
                nc.vector.tensor_tensor(stage[c][:, 1, :].bitcast(F32R), ps[:, QK_BANKS[c], :], stage[c][:, 0, :],
                                        ALU.subtract).then_inc(qlo_done, 1)

            def batch(b):
                if not first(b):
                    scale_f(b - 1, TT - 1)
                    gate_f(b - 1, TT - 1)
                for m in range(HT):
                    if m == Z_TILE and not first(b):
                        norm_z(b - 1, 1)
                    for g, k in TILE_SLOTS.get(m, ()):
                        maxima(b, g, k)
                        if k == SLOTS - 1:
                            negate(b, g)
                    hidden(b, m)
                    if m == 3 and first(b):
                        dve.wait_ge(hi_done, 5)
                        nc.vector.tensor_tensor(wdl[:].rearrange("p m n -> p (m n)"), raw_d,
                                                wdh[:].rearrange("p m n -> p (m n)").bitcast(F32),
                                                ALU.subtract).then_inc(lo_done, 1)
                    if m == 0 and not first(b):
                        invert_sums(b - 1, 1)
                    if m == 4 and not first(b):
                        finish(b - 1)
                for g in range(NG):
                    for k in range(SLOTS):
                        if g + 2 < NG:
                            maxima(b, g + 2, k)
                        if g and k == 0:
                            scale_f(b, g - 1)
                        if g and k == 3:
                            gate_f(b, g - 1)
                        if g == 1 and 5 <= k < 5 + TT and not last(b):
                            statistics(b + 1, k - 5)
                    if g + 2 < NG:
                        negate(b, g + 2)
                    if g == 2 and not last(b):
                        newton(b + 1)
                if not last(b):
                    split_x(b + 1)
                invert_sums(b, 0)
                if not last(b):
                    for c in range(3):
                        chunk_lo(b + 1, c)
                norm_z(b, 0)
                if not last(b):
                    chunk_lo(b + 1, 3)

            for i in range(TT):
                statistics(0, i)
            newton(0)
            dve.wait_ge(hi_done, 1)
            nc.vector.tensor_tensor(wl[:].rearrange("p k n -> p (k n)"), raw_qkv,
                                    wh[:].rearrange("p k n -> p (k n)").bitcast(F32),
                                    ALU.subtract).then_inc(lo_done, 1)
            split_x(0)
            for c in range(4):
                if c < 2:
                    split_gu_lo(c)
                chunk_lo(0, c)
            dve.wait_ge(hi_done, 4)
            nc.vector.tensor_tensor(wol[:].rearrange("p k n -> p (k n)"), raw_o,
                                    woh[:].rearrange("p k n -> p (k n)").bitcast(F32),
                                    ALU.subtract).then_inc(lo_done, 1)
            dve.wait_ge(sc_loaded, 32)
            nc.vector.tensor_scalar(hsg[:], sgt[:, 0, :], 0.5, None, ALU.mult).then_inc(sc_step, 1)
            dve.wait_ge(sc_step, 1)
            nc.vector.tensor_tensor(sgt[:, 2, :], hsg[:], sgt[:, 1, :], ALU.mult).then_inc(sc_step, 1)
            dve.wait_ge(sc_step, 2)
            dve.wait_ge(dve_const, 3)
            batch(0)
            with dve.Fori(1, B - 1) as b:
                batch(b)
            dve.wait_ge(consts, spare)
            batch(B - 1)
            scale_f(B - 1, TT - 1)
            gate_f(B - 1, TT - 1)
            invert_sums(B - 1, 1)
            norm_z(B - 1, 1)
            finish(B - 1)


def kernel(**inputs):
    import numpy as np
    import concourse.bacc as bacc
    from concourse.bass_utils import run_bass_kernel_spmd as run

    a = {k.replace("L0_", ""): np.asarray(v) for k, v in inputs.items()}
    pad = HIDP - HID
    arrays = {
        "x": a["attn_x"],
        "wqkvT": np.ascontiguousarray(np.concatenate([a["attn_Wq"], a["attn_Wk"], a["attn_Wv"]]).T),
        "woT": np.ascontiguousarray(a["attn_Wo"].T),
        "wgT": np.pad(a["ffn_wq_gate"].T, ((0, 0), (0, pad))),
        "wuT": np.pad(a["ffn_wq_up"].T, ((0, 0), (0, pad))),
        "wdT": np.pad(a["ffn_wq_down"].T, ((0, pad), (0, 0))),
        "sg": np.ascontiguousarray(np.pad(a["ffn_s_gate"], (0, pad)).reshape(HT, P).T),
        "su": np.ascontiguousarray(np.pad(a["ffn_s_up"], (0, pad)).reshape(HT, P).T),
        "sd": a["ffn_s_down"],
    }
    nc = bacc.Bacc("TRN2", target_bir_lowering=False, num_devices=1)
    aps = [nc.dram_tensor(f"in_{n}", v.shape, mybir.dt.from_np(v.dtype), kind="ExternalInput").ap()
           for n, v in arrays.items()]
    out = nc.dram_tensor("out_0", (B, T, D), F32, kind="ExternalOutput").ap()
    build(nc, *aps, out)
    r = run(nc, [{f"in_{n}": v for n, v in arrays.items()}], core_ids=[0])
    return r.results[0]["out_0"]
```

```python
from contextlib import ExitStack

import concourse.bass as bass
from concourse import mybir

ALU = mybir.AluOpType
ACT = mybir.ActivationFunctionType
F32 = mybir.dt.float32
F32R = mybir.dt.float32r
BF16 = mybir.dt.bfloat16
I32 = mybir.dt.int32

P = 128
B, T, D = 4, 512, 256
NH, HD = 16, 16
HID = 704
KD = D // P
TT = T // P
HT = -(-HID // P)
HIDP = HT * P
GH = 4
NG = NH // GH
HH = NH // 2
UNITS = GH * TT
SLOTS = 10
RC = T // HD
Z_TILE = 3
ROWC = 3 * HD
EPS = 1e-5
ZERO_POINT = 128.0
SCALE = float(HD) ** -0.5
NEG = -1e38
LOWEST = -3e38
MAGIC = float(0x5F3759DF)
NEWTON = 3
LN_STEPS = TT + 3 + 3 * NEWTON

SM0, SM1, ST0, ST1, BZ, GA, GB, MI = range(8)
MAX_RING = ((SM0, SM1, ST0, ST1), (SM0, SM1, GA))
ST_RING = (GB, ST0, ST1)
QK_BANKS = (GA, SM0, GA, SM1)
QK_SLOTS = (1, 3, 5, 7)

TILE_SLOTS = {m: [divmod(4 * (m - 1) + q, SLOTS) for q in range(4)] for m in range(1, HT)}


def max_bank(g, k):
    ring = MAX_RING[g // 2]
    return ring[(SLOTS * g + k) % 4] if g < 2 else ring[k % 3]


def slot_blocks(k):
    if k < GH:
        return [(k, 0, 0)]
    if k < 2 * GH:
        return [(k - GH, 1, 0), (k - GH, 3, 3 * P)]
    return [(2 * (k - 2 * GH), 2, 0), (2 * (k - 2 * GH) + 1, 2, 2 * P)]


SLOT_OF = {(a, j): (k, c) for k in range(SLOTS) for a, j, c in slot_blocks(k)}


def max_blocks(k):
    return [(a, TT - 1 - j, c) for a, j, c in slot_blocks(k)]


def build(nc, x, wqkvT, woT, wgT, wuT, wdT, sg, su, sd, out):
    with ExitStack() as ctx:
        def sb(name, shape, dt=F32):
            return ctx.enter_context(nc.sbuf_tensor(name, shape, dt))

        def sem(name):
            return ctx.enter_context(nc.semaphore(name))

        ps = ctx.enter_context(nc.psum_tensor("ps", [P, 8, 512], F32))

        qp = sb("qp", [P, NH, T], F32R)
        kp = sb("kp", [P, NH, T], F32R)
        pt = sb("pt", [P, SLOTS, T])
        vt = sb("vt", [P, TT, NH, HD + 1])
        xin = sb("xin", [P, TT, D])
        xh = sb("xh", [P, KD, T], F32R)
        xl = sb("xl", [P, KD, T], F32R)
        wh = sb("wh", [P, KD, 3 * D], F32R)
        wl = sb("wl", [P, KD, 3 * D], F32R)
        woh = sb("woh", [P, KD, D], F32R)
        wol = sb("wol", [P, KD, D], F32R)
        guh = sb("guh", [P, 2, KD, HIDP], F32R)
        gul = sb("gul", [P, 2, KD, HIDP], F32R)
        wdh = sb("wdh", [P, HT, D], F32R)
        wdl = sb("wdl", [P, HT, D], F32R)
        hh = sb("hh", [P, HT, T], F32R)
        hl = sb("hl", [P, HT, T], F32R)
        xn = sb("xn", [P, TT, D])
        zbuf = sb("zbuf", [P, 3, T])
        zs = zbuf[:, 0, :]
        zc = zbuf[:, 1, :]
        lc = zbuf[:, 2, :]
        rl = sb("rl", [P, RC])
        zh = sb("zh", [P, 2, T], F32R)
        zl = sb("zl", [P, 2, T], F32R)
        act = sb("act", [P, 2, T])
        u = sb("u", [P, TT, D])
        fth = sb("fth", [P, D])
        tri = sb("tri", [P, T], BF16)
        ident = sb("ident", [P, P])
        sdb = sb("sdb", [P, D])
        cn = sb("cn", [P, P])
        ctr = sb("ctr", [32, P], F32R)
        mx = sb("mx", [P, UNITS])
        stats = sb("stats", [P, TT, 6])
        mv = sb("mv", [P, TT, 2])
        nw = sb("nw", [P, 4, TT])
        nwi = sb("nwi", [P, 2, TT], I32)
        sgt = sb("sgt", [P, 3, HT])
        hsg = sb("hsg", [P, HT])

        qk_dram = nc.dram_tensor("qk_scratch", [2, 2, HH, 2, HD, T], F32, kind="Internal").ap()
        z_dram = nc.dram_tensor("z_scratch", [NG, P, T], F32, kind="Internal").ap()
        rl_dram = nc.dram_tensor("rl_scratch", [2, HH, T], F32, kind="Internal").ap()
        zero_dram = nc.dram_tensor("zero_scratch", [2, HH, T], F32, kind="Internal").ap()

        x_loaded = sem("x_loaded")
        wqkv_loaded, wo_loaded, gu_loaded, wd_loaded = map(
            sem, ("wqkv_loaded", "wo_loaded", "gu_loaded", "wd_loaded"))
        sc_loaded, sd_loaded, zero_stored = map(sem, ("sc_loaded", "sd_loaded", "zero_stored"))
        qk_stored = [sem(f"qk_stored_{c}") for c in range(4)]
        pack_loaded = [sem("pack_loaded_a"), sem("pack_loaded_b")]
        c_loaded = sem("c_loaded")
        z_stored = sem("z_stored")
        l_loaded = [sem("l_loaded_a"), sem("l_loaded_b")]
        rl_stored = sem("rl_stored")
        z_loaded = [sem("z_loaded_a"), sem("z_loaded_b")]
        res_loaded, out_stored = sem("res_loaded"), sem("out_stored")
        consts, pool_step, gu_float, wd_float = map(sem, ("consts", "pool_step", "gu_float", "wd_float"))
        qp_zero, kp_zero, dve_const = map(sem, ("qp_zero", "kp_zero", "dve_const"))
        kp_ones = [sem("kp_ones_a"), sem("kp_ones_b")]
        hi_done, lo_done, sc_step = map(sem, ("hi_done", "lo_done", "sc_step"))
        stats_done, ln_step, xn_done, xt_ready, xhi_done, xlo_done = map(
            sem, ("stats_done", "ln_step", "xn_done", "xt_ready", "xhi_done", "xlo_done"))
        qk_ready, qhi_done, qlo_done, v_ready, v_done = map(
            sem, ("qk_ready", "qhi_done", "qlo_done", "v_ready", "v_done"))
        gu_ready, tanh_done, up_done, gate_done, h_done, hhi_done, hlo_done = map(
            sem, ("gu_ready", "tanh_done", "up_done", "gate_done", "h_done", "hhi_done", "hlo_done"))
        f_ready, f_done, fth_done, u_done = map(sem, ("f_ready", "f_done", "fth_done", "u_done"))
        sm_ready, max_done, cn_done, ct_ready, ct_copied = map(
            sem, ("sm_ready", "max_done", "cn_done", "ct_ready", "ct_copied"))
        st_ready, exp_done, mask_done, pv_done, z_copied = map(
            sem, ("st_ready", "exp_done", "mask_done", "pv_done", "z_copied"))
        rl_done, zn_done, zhi_done, o_ready, o_used, out_done = map(
            sem, ("rl_done", "zn_done", "zhi_done", "o_ready", "o_used", "out_done"))
        zlo_done = [sem("zlo_done_a"), sem("zlo_done_b")]

        stage = [act[:], xn[:].rearrange("p i d -> p (i d)").rearrange("p (s n) -> p s n", s=2),
                 hl[:, HT - 2:, :].bitcast(F32), hh[:, HT - 2:, :].bitcast(F32)]
        up = [pt[:, SLOTS - 2 + n, :] for n in range(2)]
        flat = pt[:].rearrange("p s n -> p (s n)")
        n_qkv, n_o, n_gu = KD * 3 * D, KD * D, 2 * KD * HIDP
        raw_qkv = flat[:, 0:n_qkv]
        raw_o = flat[:, n_qkv:n_qkv + n_o]
        raw_gu = flat[:, n_qkv + n_o:n_qkv + n_o + n_gu]
        raw_d = zbuf[:].rearrange("p a n -> p (a n)")

        def first(b):
            return isinstance(b, int) and b == 0

        def last(b):
            return isinstance(b, int) and b == B - 1

        def out_bank(b, i):
            return ps[:, i, 0:D] if last(b) else ps[:, SM0 + i // 2, (i % 2) * D:(i % 2 + 1) * D]

        def carry(engine, register):
            engine.reg_alu(register, register, 1, ALU.bitwise_or)

        block = ctx.enter_context(nc.Block())

        @block.sync
        def _(sp):
            sp.dma_start(xin[:], x[0].rearrange("(i p) d -> p i d", p=P)).then_inc(x_loaded, 16)
            sp.dma_start(raw_qkv.rearrange("p (k n) -> p k n", k=KD),
                         wqkvT.rearrange("(k p) n -> p k n", p=P)).then_inc(wqkv_loaded, 16)
            g4 = raw_gu.bitcast(I32).rearrange("p (w k n) -> p w k n", w=2, k=KD)
            sp.dma_start(g4[:, 0], wgT.rearrange("(k p) n -> p k n", p=P)).then_inc(gu_loaded, 16)
            sp.dma_start(g4[:, 1], wuT.rearrange("(k p) n -> p k n", p=P)).then_inc(gu_loaded, 16)
            sp.dma_start(raw_o.rearrange("p (k n) -> p k n", k=KD),
                         woT.rearrange("(k p) n -> p k n", p=P)).then_inc(wo_loaded, 16)
            sp.dma_start(sgt[:, 0, :], sg).then_inc(sc_loaded, 16)
            sp.dma_start(sgt[:, 1, :], su).then_inc(sc_loaded, 16)
            sp.dma_start(sdb[:], sd.rearrange("(a d) -> a d", a=1).to_broadcast([P, D])).then_inc(sd_loaded, 16)
            sp.dma_start(raw_d.bitcast(I32).rearrange("p (m n) -> p m n", m=HT),
                         wdT.rearrange("(m p) n -> p m n", p=P)).then_inc(wd_loaded, 16)
            sp.wait_ge(qp_zero, 1)
            sp.dma_start(zero_dram, qp[64:66, 0:HH, :].bitcast(F32)).then_inc(zero_stored, 16)
            sp.wait_ge(dve_const, 1)
            sp.wait_ge(zero_stored, 16)

            def store_qk(b, c):
                sp.wait_ge(qlo_done, 4 * b + c + 1)
                for s in range(2):
                    sp.dma_start(qk_dram[c % 2, c // 2, :, s], stage[c][:, s, :]).then_inc(qk_stored[c], 16)

            def k_ones(half):
                sp.wait_ge(qp_zero, half + 1)
                sp.wait_ge(kp_zero, half + 1)
                sp.dma_start(kp[ROWC:ROWC + 2, HH * half:HH * (half + 1), :].bitcast(F32),
                             u[0:HH, :, :]).then_inc(kp_ones[half], 16)

            def store_z(b, g):
                sp.wait_ge(z_copied, NG * b + g + 1)
                load_sums(b, g)
                sp.dma_start(z_dram[g], zs).then_inc(z_stored, 16)

            def z_in_scratch(b, g):
                sp.wait_ge(z_stored, 16 * (NG * b + g + 1))

            def load_z(b, g):
                half, part = g // 2, 64 * (g % 2)
                if g == 0 and not first(b):
                    sp.wait_ge(zlo_done[1], b)
                if g == 2:
                    sp.wait_ge(zlo_done[0], b + 1)
                rows = z_dram[g].rearrange("(a r) n -> a r n", a=GH)
                sp.dma_start(zbuf[part:part + 64, 1, :], rows[:, 0:HD, :]).then_inc(z_loaded[half], 16)

            def load_sums(b, g):
                half, part = g // 2, 64 * (g % 2)
                if g == 2:
                    sp.wait_ge(rl_stored, 16 * (2 * b + 1))
                elif g == 0 and not first(b):
                    sp.wait_ge(rl_stored, 32 * b)
                sp.dma_start(rl[part:part + 64, :], zbuf[HD::32, 0, :]).then_inc(l_loaded[half], 16)

            def store_rl(b, half):
                sp.wait_ge(rl_done, 2 * b + half + 1)
                sp.dma_start(rl_dram[half], rl[:]).then_inc(rl_stored, 16)

            def load_rl(b, half):
                sp.wait_ge(rl_stored, 16 * (2 * b + half + 1))
                sp.dma_start(lc, rl_dram[half].rearrange("h (o n) -> h o n", o=1).to_broadcast([HH, HD, T])
                             ).then_inc(z_loaded[half], 16)

            def c_rows(b, g):
                sp.wait_ge(ct_copied, NG * b + g + 1)
                sp.dma_start(qp[ROWC:ROWC + 2, GH * g:GH * (g + 1), :].bitcast(F32),
                             ctr[:].bitcast(F32)).then_inc(c_loaded, 16)

            def store_out(b, p):
                sp.wait_ge(out_done, 2 * b + p + 1)
                sp.dma_start(out[b].rearrange("(i p) d -> p i d", p=P)[:, 2 * p:2 * p + 2, :],
                             xin[:, 2 * p:2 * p + 2, :]).then_inc(out_stored, 16)

            def stack(b, half, ws=(0, 1)):
                heads = slice(HH * half, HH * (half + 1))
                for w in ws:
                    buf, both, again = ((qp, 0, 2 * HD), (kp, HD, 0))[w]
                    sp.wait_ge(qk_stored[2 * half + w], 32 * (b + 1))
                    sp.dma_start(buf[both:both + 2 * HD, heads, :].bitcast(F32),
                                 qk_dram[w, half].rearrange("h s d n -> (s d) h n")).then_inc(pack_loaded[half], 16)
                    sp.dma_start(buf[again:again + HD, heads, :].bitcast(F32),
                                 qk_dram[w, half, :, 0].rearrange("h d n -> d h n")).then_inc(pack_loaded[half], 16)
                    if w == 0:
                        sp.dma_start(qp[ROWC:ROWC + 2, heads, :].bitcast(F32), zero_dram).then_inc(pack_loaded[half], 16)

            def batch(b):
                if not first(b):
                    store_z(b - 1, 3)
                    store_rl(b - 1, 1)
                    z_in_scratch(b - 1, 3)
                    load_z(b - 1, 2)
                    load_z(b - 1, 3)
                    load_rl(b - 1, 1)
                stack(b, 1)
                c_rows(b, 0)
                if first(b):
                    sp.wait_ge(xn_done, TT)
                else:
                    store_out(b - 1, 0)
                    store_out(b - 1, 1)
                    sp.wait_ge(out_stored, 32 * b)
                sp.dma_start(xin[:], x[B - 1 if last(b) else b + 1].rearrange("(i p) d -> p i d", p=P)
                             ).then_inc(x_loaded, 16)
                c_rows(b, 1)
                c_rows(b, 2)
                store_z(b, 0)
                z_in_scratch(b, 0)
                load_z(b, 0)
                c_rows(b, 3)
                store_z(b, 1)
                z_in_scratch(b, 1)
                load_z(b, 1)
                if not last(b):
                    sp.wait_ge(xn_done, TT * (b + 2))
                    sp.dma_start(xin[:], x[b].rearrange("(i p) d -> p i d", p=P)).then_inc(res_loaded, 16)
                store_rl(b, 0)
                if not last(b):
                    store_qk(b + 1, 0)
                load_rl(b, 0)
                if not last(b):
                    store_qk(b + 1, 1)
                    stack(b + 1, 0, (0,))
                store_z(b, 2)
                if not last(b):
                    store_qk(b + 1, 2)
                    stack(b + 1, 0, (1,))
                    store_qk(b + 1, 3)

            k_ones(0)
            store_qk(0, 0)
            store_qk(0, 1)
            stack(0, 0)
            store_qk(0, 2)
            store_qk(0, 3)
            k_ones(1)
            batch(0)
            with sp.Fori(1, B - 1) as b:
                batch(b)
            batch(B - 1)
            store_z(B - 1, 3)
            store_rl(B - 1, 1)
            z_in_scratch(B - 1, 3)
            load_z(B - 1, 2)
            load_z(B - 1, 3)
            load_rl(B - 1, 1)
            store_out(B - 1, 0)
            store_out(B - 1, 1)
            sp.wait_ge(out_stored, 32 * B)

        @block.tensor
        def _(pe):
            def split3(dst, lh, ll, rh, rl, start, stop):
                nc.tensor.matmul(dst, lh, rh, start=start, stop=False)
                nc.tensor.matmul(dst, lh, rl, start=False, stop=False)
                return nc.tensor.matmul(dst, ll, rh, start=False, stop=stop)

            def transpose_x(b):
                pe.wait_ge(xn_done, TT * (b + 1))
                if not first(b):
                    pe.wait_ge(max_done, NG * SLOTS * b)
                for k in range(KD):
                    for i in range(TT):
                        mm = nc.tensor.transpose(ps[:, SM0 + k, i * P:(i + 1) * P],
                                                 xn[:, i, k * P:(k + 1) * P], ident[:])
                    mm.then_inc(xt_ready, 1)

            def project_qk(b, c):
                if c == 0:
                    pe.wait_ge(xlo_done, KD * (b + 1))
                    if first(b):
                        pe.wait_ge(hi_done, 1)
                        pe.wait_ge(lo_done, 1)
                if c == 2:
                    pe.wait_ge(qlo_done, 4 * b + 1)
                col = (c % 2) * D + (c // 2) * P
                for k in range(KD):
                    mm = split3(ps[:, QK_BANKS[c], :], wh[:, k, col:col + P], wl[:, k, col:col + P],
                                xh[:, k, :], xl[:, k, :], k == 0, k == KD - 1)
                mm.then_inc(qk_ready, 1)

            def project_v(b):
                for n in range(2):
                    for i in (2 * n, 2 * n + 1):
                        for k in range(KD):
                            rows = slice(i * P, (i + 1) * P)
                            dst = ps[:, ST0 + n, (i % 2) * D:(i % 2 + 1) * D]
                            mm = split3(dst, xh[:, k, rows], xl[:, k, rows], wh[:, k, 2 * D:], wl[:, k, 2 * D:],
                                        k == 0, k == KD - 1)
                    mm.then_inc(v_ready, 1)

            def gate_up(b, m, between=None):
                banks = (GA, GB) if m % 2 == 0 else (MI, BZ)
                if m == 0:
                    pe.wait_ge(qlo_done, 4 * b + 3)
                if m == 1 and not first(b):
                    pe.wait_ge(f_done, TT * b)
                if m >= 2:
                    pe.wait_ge(gate_done, HT * b + m - 1)
                    pe.wait_ge(up_done, HT * b + m - 1)
                cols = slice(m * P, (m + 1) * P)
                for w in range(2):
                    if m == 0 and first(b):
                        pe.wait_ge(hi_done, 2 + w)
                        pe.wait_ge(lo_done, 2 + w)
                    if w == 1 and m == 0 and not first(b):
                        pe.wait_ge(exp_done, NG * SLOTS * b)
                    if w == 1 and m == 1 and not first(b):
                        pe.wait_ge(z_copied, NG * b)
                    if w == 1 and m == HT - 1:
                        pe.wait_ge(ct_copied, NG * b + 1)
                    for k in range(KD):
                        mm = split3(ps[:, banks[w], :], guh[:, w, k, cols], gul[:, w, k, cols],
                                    xh[:, k, :], xl[:, k, :], k == 0, k == KD - 1)
                        if between and (w, k) != (1, 1):
                            between(2 * w + k)
                mm.then_inc(gu_ready, 1)
                if between:
                    between(3)

            def maxima_slot(b, g, k):
                if k == 0 and g % 2 == 0:
                    pe.wait_ge(pack_loaded[g // 2], 16 * 5 * (b + 1))
                if k == 0 and first(b) and g % 2 == 0:
                    pe.wait_ge(kp_ones[g // 2], 16)
                n = SLOTS * g + k
                if g == 0 and k == 1:
                    pe.wait_ge(qlo_done, 4 * b + 4)
                if g == 0 and k == 2:
                    pe.wait_ge(v_done, 2 * b + 2)
                if g == 1 and k in (6, 7) and not first(b):
                    pe.wait_ge(o_used, 2 * (b - 1) + k - 5)
                if g == 2 and k == 2:
                    pe.wait_ge(gate_done, HT * b + 5)
                before = [m for m in range(n) if max_bank(*divmod(m, SLOTS)) == max_bank(g, k)]
                if before:
                    pe.wait_ge(max_done, NG * SLOTS * b + before[-1] + 1)
                for a, i, c in max_blocks(k):
                    h, w = GH * g + a, (i + 1) * P
                    mm = nc.tensor.matmul(ps[:, max_bank(g, k), c:c + w], qp[:, h, i * P:(i + 1) * P],
                                          kp[:, h, 0:w], start=True, stop=True)
                mm.then_inc(sm_ready, 1)

            def transpose_c(b, g):
                pe.wait_ge(cn_done, 2 * (NG * b + g + 1))
                if g == 0:
                    pe.wait_ge(up_done, HT * b + 4)
                elif g == 1:
                    pe.wait_ge(gate_done, HT * b + HT)
                else:
                    pe.wait_ge(f_done, TT * b + g - 1)
                dst = ps[:, BZ, 0:P] if g == 0 else ps[:, MI, 0:P]
                nc.tensor.transpose(dst, cn[:], ident[:]).then_inc(ct_ready, 1)

            def project_out(b):
                for half in range(2):
                    pe.wait_ge(zlo_done[half], b + 1)
                pe.wait_ge(max_done, NG * SLOTS * (b + 1) + 14)
                for i in range(TT):
                    for k in range(2):
                        rows = slice(i * P, (i + 1) * P)
                        mm = split3(out_bank(b, i), zh[:, k, rows], zl[:, k, rows], woh[:, k, :], wol[:, k, :],
                                    k == 0, k == 1)
                    if i % 2 == 1:
                        mm.then_inc(o_ready, 1)

            def project_last_out(b):
                pe.wait_ge(exp_done, NG * SLOTS * B)
                for k in range(2):
                    pe.wait_ge(zlo_done[k], b + 1)
                    for i in range(TT):
                        rows = slice(i * P, (i + 1) * P)
                        mm = split3(out_bank(b, i), zh[:, k, rows], zl[:, k, rows], woh[:, k, :], wol[:, k, :],
                                    k == 0, k == 1)
                        if k == 1 and i % 2 == 1:
                            mm.then_inc(o_ready, 1)

            def scores_slot(b, g, k):
                if k == 0:
                    pe.wait_ge(c_loaded, 16 * (NG * b + g + 1))
                n = SLOTS * g + k
                if n == 0:
                    pe.wait_ge(up_done, HT * b + 5)
                elif n < 3:
                    pe.wait_ge(max_done, NG * SLOTS * b + 2 * SLOTS - 2 + n)
                else:
                    pe.wait_ge(exp_done, NG * SLOTS * b + n - 2)
                blocks = slot_blocks(k)
                for a, j, c in blocks:
                    h = GH * g + a
                    mm = nc.tensor.matmul(ps[:, ST_RING[n % 3], c:c + T - j * P], kp[:, h, j * P:(j + 1) * P],
                                          qp[:, h, j * P:], start=True, stop=True)
                mm.then_inc(st_ready, 1)

            def values(b, g, js, stage):
                if js[0] == 0 and g == 0:
                    pe.wait_ge(up_done, HT * (b + 1))
                elif js[0] == 0:
                    pe.wait_ge(z_copied, NG * b + g)
                pe.wait_ge(mask_done, SLOTS * (NG * b + g) + (4, 8, 10)[stage])
                for j in js:
                    for a in range(GH):
                        k, c = SLOT_OF[a, j]
                        mm = nc.tensor.matmul(ps[32 * a:32 * a + HD + 1, BZ, j * P:],
                                              vt[:, j, GH * g + a, :], pt[:, k, c:c + T - j * P],
                                              start=(j == 0), stop=(j == 2))
                mm.then_inc(pv_done, 1)

            def project_down(b, i, ms):
                if ms[0] == 0 and i == 0:
                    pe.wait_ge(hlo_done, HT * (b + 1))
                    if first(b):
                        pe.wait_ge(hi_done, 5)
                        pe.wait_ge(lo_done, 5)
                elif ms[0] == 0:
                    pe.wait_ge(f_done, TT * b + i)
                if ms[0] == 0 and i + 1 < NG:
                    pe.wait_ge(ct_copied, NG * b + i + 2)
                rows = slice(i * P, (i + 1) * P)
                for m in ms:
                    mm = split3(ps[:, MI, 0:D], hh[:, m, rows], hl[:, m, rows], wdh[:, m, :], wdl[:, m, :],
                                m == 0, m == HT - 1)
                if ms[-1] == HT - 1:
                    mm.then_inc(f_ready, 1)

            def batch(b):
                def last_values(q):
                    if q == 0:
                        values(b - 1, 3, (1, 3), 1)
                    if q == 1:
                        values(b - 1, 3, (2,), 2)

                gate_up(b, 0, None if first(b) else last_values)
                project_v(b)
                for m in range(1, HT):
                    gate_up(b, m, lambda q: maxima_slot(b, *TILE_SLOTS[m][q]))
                    if m == HT - 2:
                        if not first(b):
                            project_out(b - 1)
                        transpose_c(b, 0)
                for g in range(NG):
                    for k in range(SLOTS):
                        scores_slot(b, g, k)
                        if g + 2 < NG:
                            maxima_slot(b, g + 2, k)
                        if g and k == 1:
                            values(b, g - 1, (1, 3), 1)
                        if k == 2 and g + 1 < NG:
                            transpose_c(b, g + 1)
                        if g == 0 and k >= 5:
                            project_down(b, g, (4, 5) if k == 9 else (k - 5,))
                        if g in (1, 2) and k >= 4:
                            project_down(b, g, (k - 4,))
                        if g == 3 and k < 3:
                            project_down(b, g, (2 * k, 2 * k + 1))
                        if g and k == 4:
                            values(b, g - 1, (2,), 2)
                        if not last(b) and g == 3 and k in QK_SLOTS:
                            project_qk(b + 1, QK_SLOTS.index(k))
                        if g == 2 and k == 8 and not last(b):
                            transpose_x(b + 1)
                    values(b, g, (0,), 0)

            pe.wait_ge(consts, 2)
            transpose_x(0)
            for c in range(4):
                project_qk(0, c)
            batch(0)
            with pe.Fori(1, B - 1) as b:
                batch(b)
            batch(B - 1)
            values(B - 1, 3, (1, 3), 1)
            values(B - 1, 3, (2,), 2)
            project_last_out(B - 1)

        @block.scalar
        def _(act_e):
            act_e.wait_ge(wqkv_loaded, 16)
            nc.scalar.copy(wh[:].rearrange("p k n -> p (k n)"), raw_qkv).then_inc(hi_done, 1)
            def split_gu_hi(w):
                act_e.wait_ge(gu_float, w + 1)
                nc.scalar.copy(guh[:, w].rearrange("p k n -> p (k n)"),
                               raw_gu[:, w * KD * HIDP:(w + 1) * KD * HIDP]).then_inc(hi_done, 1)

            def split_x(b):
                for k in range(KD):
                    act_e.wait_ge(xt_ready, KD * b + k + 1)
                    if k == 0 and not first(b):
                        act_e.wait_ge(v_ready, 2 * b)
                        act_e.wait_ge(gu_ready, HT * b)
                    nc.scalar.copy(xh[:, k, :], ps[:, SM0 + k, :]).then_inc(xhi_done, 1)

            def chunk_hi(b, c):
                act_e.wait_ge(qk_ready, 4 * b + c + 1)
                if c < 2 and not first(b):
                    act_e.wait_ge(pack_loaded[0], 80 * b)
                    act_e.wait_ge(pack_loaded[1], 80 * b)
                if c == 0 and not first(b):
                    act_e.wait_ge(hlo_done, HT * b)
                if c == 1:
                    act_e.wait_ge(xt_ready, KD * (b + 1))
                if c == 2 and not first(b):
                    act_e.wait_ge(f_ready, TT * b)
                nc.scalar.copy(stage[c][:, 0, :].bitcast(F32R), ps[:, QK_BANKS[c], :]).then_inc(qhi_done, 1)

            def hidden_hi(b, m):
                act_e.wait_ge(h_done, HT * b + m + 1)
                if m == 0 and not first(b):
                    act_e.wait_ge(f_ready, TT * b)
                if m == HT - 2:
                    act_e.wait_ge(qk_stored[2], 32 * (b + 1))
                    act_e.wait_ge(qk_stored[3], 32 * (b + 1))
                nc.scalar.copy(hh[:, m, :], act[:, m % 2, :]).then_inc(hhi_done, 1)

            def z_hi(b, half):
                act_e.wait_ge(zn_done, 2 * b + half + 1)
                if half == 0 and not first(b):
                    act_e.wait_ge(o_ready, 2 * b)
                nc.scalar.copy(zh[:, half, :], zc).then_inc(zhi_done, 1)

            def copy_c(b, g):
                n = NG * b + g + 1
                act_e.wait_ge(ct_ready, n)
                if g or not first(b):
                    act_e.wait_ge(c_loaded, 16 * (n - 1))
                src = ps[0:32, BZ, 0:P] if g == 0 else ps[0:32, MI, 0:P]
                nc.scalar.copy(ctr[:], src).then_inc(ct_copied, 1)

            def copy_z(b, g):
                act_e.wait_ge(pv_done, 3 * (NG * b + g + 1))
                if g or not first(b):
                    act_e.wait_ge(z_stored, 16 * (NG * b + g))
                    act_e.wait_ge(l_loaded[(g - 1) % 4 // 2], 32 * b + 16 * ((g - 1) % 2 + 1) if g else 32 * b)
                nc.scalar.copy(zs, ps[:, BZ, :]).then_inc(z_copied, 1)

            def ffn_tanh(b, i):
                act_e.wait_ge(f_done, TT * b + i + 1)
                if i or not first(b):
                    act_e.wait_ge(u_done, TT * b + i)
                nc.scalar.activation(fth[:], u[:, i, :], ACT.Tanh, scale=0.5).then_inc(fth_done, 1)

            def batch(b):
                if not first(b):
                    ffn_tanh(b - 1, TT - 1)
                    copy_z(b - 1, NG - 1)
                for m in range(HT):
                    act_e.wait_ge(gu_ready, HT * b + m + 1)
                    if m >= 2:
                        act_e.wait_ge(hlo_done, HT * b + m - 1)
                    if m == 0:
                        act_e.wait_ge(qk_stored[0], 32 * (b + 1))
                    if m == 0 and first(b):
                        act_e.wait_ge(sc_step, 1)
                    gbank = GA if m % 2 == 0 else MI
                    nc.scalar.activation(act[:, m % 2, :], ps[:, gbank, :], ACT.Tanh,
                                         scale=hsg[:, m:m + 1]).then_inc(tanh_done, 1)
                    ubank = GB if m % 2 == 0 else BZ
                    if m == 0 and first(b):
                        act_e.wait_ge(sc_step, 2)
                        act_e.wait_ge(lo_done, 3)
                    nc.scalar.activation(up[m % 2], ps[:, ubank, :], ACT.Copy,
                                         scale=sgt[:, 2, m:m + 1]).then_inc(up_done, 1)
                    if m == 0:
                        for n in range(2):
                            act_e.wait_ge(v_ready, 2 * b + n + 1)
                            nc.scalar.copy(vt[:, 2 * n:2 * n + 2, :, 0:HD],
                                           ps[:, ST0 + n, :].rearrange("p (i h d) -> p i h d", i=2, d=HD)
                                           ).then_inc(v_done, 1)
                    if m == HT - 2:
                        copy_c(b, 0)
                    if m < HT - 1:
                        hidden_hi(b, m)
                    if m == Z_TILE - 1 and not first(b):
                        z_hi(b - 1, 1)
                if first(b):
                    act_e.wait_ge(lo_done, 5)
                for g in range(NG):
                    for k in range(SLOTS):
                        act_e.wait_ge(st_ready, SLOTS * (NG * b + g) + k + 1)
                        if k in (0, 4, 8) and not (first(b) and g == 0):
                            act_e.wait_ge(pv_done, 3 * (NG * b + g) - 2 + k // 4)
                        nc.scalar.activation(pt[:, k, :], ps[:, ST_RING[(SLOTS * g + k) % 3], :], ACT.Exp,
                                             scale=SCALE).then_inc(exp_done, 1)
                        if k == 1 and g:
                            ffn_tanh(b, g - 1)
                        if g == 0 and k == 1:
                            hidden_hi(b, HT - 1)
                        if k == 2 and g + 1 < NG:
                            copy_c(b, g + 1)
                        if g == 2 and k == 8 and not last(b):
                            split_x(b + 1)
                        if k == 5 and g:
                            copy_z(b, g - 1)
                        if g == 3 and not last(b):
                            if k - 1 in QK_SLOTS:
                                chunk_hi(b + 1, QK_SLOTS.index(k - 1))
                z_hi(b, 0)

            split_x(0)
            for c in range(4):
                if c == 0:
                    split_gu_hi(0)
                    split_gu_hi(1)
                chunk_hi(0, c)
            act_e.wait_ge(wo_loaded, 16)
            nc.scalar.copy(woh[:].rearrange("p k n -> p (k n)"), raw_o).then_inc(hi_done, 1)
            act_e.wait_ge(wd_float, 1)
            nc.scalar.copy(wdh[:].rearrange("p m n -> p (m n)"), raw_d).then_inc(hi_done, 1)
            batch(0)
            with act_e.Fori(1, B - 1) as b:
                batch(b)
            batch(B - 1)
            ffn_tanh(B - 1, TT - 1)
            copy_z(B - 1, NG - 1)
            z_hi(B - 1, 1)

        @block.gpsimd
        def _(pool):
            spare = pool.alloc_register("pool_spare")
            pool.reg_mov(spare, 1)
            nc.gpsimd.memset(ident[:], 0.0).then_inc(pool_step, 1)
            nc.gpsimd.memset(tri[:], 0.0).then_inc(pool_step, 1)
            pool.wait_ge(pool_step, 2)
            nc.gpsimd.affine_select(out=ident[:], in_=ident[:], compare_op=ALU.not_equal, fill=1.0, base=0,
                                    pattern=[[-1, P]], channel_multiplier=1).then_inc(consts, 1)
            nc.gpsimd.affine_select(out=tri[:, T - P:], in_=tri[:, T - P:], compare_op=ALU.is_ge, fill=NEG,
                                    base=0, pattern=[[-1, P]], channel_multiplier=1).then_inc(consts, 1)
            pool.wait_ge(consts, 2)
            for half in range(2):
                heads = slice(HH * half, HH * (half + 1))
                nc.gpsimd.memset(qp[:, heads, :].bitcast(F32), 0.0).then_inc(qp_zero, 1)
                nc.gpsimd.memset(kp[:, heads, :].bitcast(F32), 0.0).then_inc(kp_zero, 1)
                if half == 0:
                    for w in range(2):
                        pool.wait_ge(gu_loaded, 32)
                        part = raw_gu[:, w * KD * HIDP:(w + 1) * KD * HIDP]
                        nc.gpsimd.tensor_scalar(part, part.bitcast(I32), -ZERO_POINT, 1.0,
                                                ALU.add, ALU.mult).then_inc(gu_float, 1)
            pool.wait_ge(qp_zero, 2)
            pool.wait_ge(kp_zero, 2)
            pool.wait_ge(gu_float, 2)
            pool.wait_ge(wd_loaded, 16)
            nc.gpsimd.tensor_scalar(raw_d, raw_d.bitcast(I32), -ZERO_POINT, 1.0, ALU.add, ALU.mult).then_inc(wd_float, 1)

            def split_z(b, half):
                n = 2 * b + half
                pool.wait_ge(zhi_done, n + 1)
                nc.gpsimd.tensor_tensor(zl[:, half, :], zc, zh[:, half, :].bitcast(F32),
                                        ALU.subtract).then_inc(zlo_done[half], 1)

            def residual(b):
                for n in range(2):
                    if n == 0:
                        pool.wait_ge(res_loaded, 16 * (b + 1))
                    pool.wait_ge(o_used, 2 * b + n + 1)
                    part = xin[:, 2 * n:2 * n + 2, :]
                    nc.gpsimd.tensor_tensor(part, part, u[:, 2 * n:2 * n + 2, :], ALU.add).then_inc(out_done, 1)

            def batch(b):
                for m in range(HT):
                    if m == Z_TILE and not first(b):
                        split_z(b - 1, 1)
                    a = act[:, m % 2, :]
                    pool.wait_ge(up_done, HT * b + m + 1)
                    pool.wait_ge(gate_done, HT * b + m + 1)
                    nc.gpsimd.tensor_tensor(a, a, up[m % 2], ALU.mult).then_inc(h_done, 1)
                    pool.wait_ge(hhi_done, HT * b + m + 1)
                    nc.gpsimd.tensor_tensor(hl[:, m, :], a, hh[:, m, :].bitcast(F32),
                                            ALU.subtract).then_inc(hlo_done, 1)
                    if m == 4 and not first(b):
                        residual(b - 1)
                for g in range(NG):
                    for k in range(SLOTS):
                        pool.wait_ge(exp_done, SLOTS * (NG * b + g) + k + 1)
                        blocks = pt[:, k, :].rearrange("p (a c) -> p a c", c=P)
                        step = (4, 3, 2)[k // GH]
                        diag = blocks[:, 0:4:step, :] if k >= GH else blocks[:, 0:1, :]
                        carry(pool, spare)
                        nc.gpsimd.affine_select(out=diag, in_=diag, compare_op=ALU.is_ge, fill=0.0, base=0,
                                                pattern=[[0, diag.shape[1]], [1, P]],
                                                channel_multiplier=-1).then_inc(mask_done, 1)
                split_z(b, 0)

            batch(0)
            with pool.Fori(1, B - 1) as b:
                batch(b)
            batch(B - 1)
            pool.wait_ge(consts, spare)

        @block.vector
        def _(dve):
            spare = dve.alloc_register("dve_spare")
            dve.reg_mov(spare, 1)
            nc.vector.memset(u[0:HD, :, :], 1.0).then_inc(dve_const, 1)
            nc.vector.memset(vt[:, :, :, HD:HD + 1], 1.0).then_inc(dve_const, 1)
            nc.vector.memset(cn[:], 0.0).then_inc(dve_const, 1)

            def statistics(b, i):
                if i == 0:
                    dve.wait_ge(x_loaded, 16 * (b + 1))
                nc.vector.bn_stats(stats[:, i, :], xin[:, i, :]).then_inc(stats_done, 1)

            def newton(b):
                s = [LN_STEPS * b]

                def step(ins, wait=True):
                    s[0] = s[0] + 1
                    ins.then_inc(ln_step, 1)
                    if wait:
                        dve.wait_ge(ln_step, s[0])

                dve.wait_ge(stats_done, TT * (b + 1))
                carry(dve, spare)
                for i in range(TT):
                    step(nc.vector.bn_aggr(mv[:, i, :], stats[:, i, :]), i == TT - 1)
                v, y, t = nw[:, 0, :], nw[:, 1, :], nw[:, 2, :]
                step(nc.vector.tensor_scalar(v, mv[:, :, 1], EPS, None, ALU.add))
                step(nc.vector.tensor_scalar(nwi[:, 0, :], v.bitcast(I32), 1, None, ALU.logical_shift_right))
                step(nc.vector.tensor_scalar(y.bitcast(I32), nwi[:, 0, :], -1.0, MAGIC, ALU.mult, ALU.add))
                for _ in range(NEWTON):
                    step(nc.vector.tensor_tensor(t, y, y, ALU.mult))
                    step(nc.vector.scalar_tensor_tensor(t, t, -0.5, v, ALU.mult, ALU.mult))
                    step(nc.vector.scalar_tensor_tensor(y, t, 1.5, y, ALU.add, ALU.mult))
                if not first(b):
                    dve.wait_ge(qk_stored[1], 32 * b)
                for i in range(TT):
                    nc.vector.tensor_scalar(xn[:, i, :], xin[:, i, :], mv[:, i, 0:1], nw[:, 1, i:i + 1],
                                            ALU.subtract, ALU.mult).then_inc(xn_done, 1)

            def split_gu_lo(w):
                dve.wait_ge(hi_done, 2 + w)
                nc.vector.tensor_tensor(gul[:, w].rearrange("p k n -> p (k n)"),
                                        raw_gu[:, w * KD * HIDP:(w + 1) * KD * HIDP],
                                        guh[:, w].rearrange("p k n -> p (k n)").bitcast(F32),
                                        ALU.subtract).then_inc(lo_done, 1)

            def invert_sums(b, half):
                if half or not first(b):
                    dve.wait_ge(zn_done, 2 * b + half)
                dve.wait_ge(l_loaded[half], 32 * (b + 1))
                nc.vector.reciprocal(rl[:], rl[:]).then_inc(rl_done, 1)

            def norm_z(b, half):
                dve.wait_ge(z_loaded[half], 48 * (b + 1))
                nc.vector.tensor_tensor(zc, zc, lc, ALU.mult).then_inc(zn_done, 1)

            def hidden(b, m):
                gbank = GA if m % 2 == 0 else MI
                a = act[:, m % 2, :]
                n = HT * b + m + 1
                dve.wait_ge(tanh_done, n)
                nc.vector.scalar_tensor_tensor(a, a, 1.0, ps[:, gbank, :], ALU.add, ALU.mult).then_inc(gate_done, 1)

            def maxima(b, g, k):
                dve.wait_ge(sm_ready, SLOTS * (NG * b + g) + k + 1)
                if k == 0 and (g or not first(b)):
                    dve.wait_ge(cn_done, 2 * (NG * b + g))
                carry(dve, spare)
                for a, i, c in max_blocks(k):
                    w = (i + 1) * P
                    s = ps[:, max_bank(g, k), c:c + w]
                    n = TT * a + i
                    mm = nc.vector.tensor_tensor_reduce(s, s, tri[:, T - w:], 1.0, LOWEST, ALU.add, ALU.max,
                                                        mx[:, n:n + 1])
                mm.then_inc(max_done, 1)

            def negate(b, g):
                n = NG * b + g + 1
                dve.wait_ge(max_done, SLOTS * n)
                if g or not first(b):
                    dve.wait_ge(ct_ready, n - 1)
                nc.vector.tensor_scalar(cn[:, 0:UNITS].bitcast(F32R), mx[:], -1.0, None, ALU.mult).then_inc(cn_done, 1)
                dve.wait_ge(cn_done, 2 * n - 1)
                nc.vector.scalar_tensor_tensor(cn[:, UNITS:2 * UNITS], mx[:], -1.0, cn[:, 0:UNITS],
                                               ALU.mult, ALU.subtract).then_inc(cn_done, 1)

            def finish(b, parts=(0, 1)):
                for n in parts:
                    k = 2 * b + n + 1
                    dve.wait_ge(o_ready, k)
                    un = u[:, 2 * n:2 * n + 2, :]
                    so = ps[:, 2 * n:2 * n + 2, 0:D] if last(b) else ps[:, SM0 + n, :].rearrange("p (i d) -> p i d", i=2)
                    nc.vector.scalar_tensor_tensor(un, so, 0.5, un,
                                                   ALU.mult, ALU.mult).then_inc(o_used, 1)

            def scale_f(b, i):
                dve.wait_ge(f_ready, TT * b + i + 1)
                if i == 0:
                    if first(b):
                        dve.wait_ge(sd_loaded, 16)
                        dve.wait_ge(kp_ones[0], 16)
                        dve.wait_ge(kp_ones[1], 16)
                    else:
                        dve.wait_ge(out_done, 2 * b)
                nc.vector.tensor_tensor(u[:, i, :], ps[:, MI, 0:D], sdb[:], ALU.mult).then_inc(f_done, 1)

            def gate_f(b, i):
                dve.wait_ge(fth_done, TT * b + i + 1)
                nc.vector.scalar_tensor_tensor(u[:, i, :], fth[:], 1.0, u[:, i, :],
                                               ALU.add, ALU.mult).then_inc(u_done, 1)

            def split_x(b):
                for k in range(KD):
                    dve.wait_ge(xhi_done, KD * b + k + 1)
                    nc.vector.tensor_tensor(xl[:, k, :], ps[:, SM0 + k, :], xh[:, k, :].bitcast(F32),
                                            ALU.subtract).then_inc(xlo_done, 1)

            def chunk_lo(b, c):
                dve.wait_ge(qhi_done, 4 * b + c + 1)
                nc.vector.tensor_tensor(stage[c][:, 1, :].bitcast(F32R), ps[:, QK_BANKS[c], :], stage[c][:, 0, :],
                                        ALU.subtract).then_inc(qlo_done, 1)

            def batch(b):
                if not first(b):
                    scale_f(b - 1, TT - 1)
                    gate_f(b - 1, TT - 1)
                for m in range(HT):
                    if m == Z_TILE and not first(b):
                        norm_z(b - 1, 1)
                    for g, k in TILE_SLOTS.get(m, ()):
                        maxima(b, g, k)
                        if k == SLOTS - 1 and g == 0:
                            negate(b, 0)
                    hidden(b, m)
                    if m == HT - 1:
                        negate(b, 1)
                    if m == 0 and not first(b):
                        invert_sums(b - 1, 1)
                    if m == 4 and not first(b):
                        finish(b - 1)
                for g in range(NG):
                    for k in range(SLOTS):
                        if g + 2 < NG:
                            maxima(b, g + 2, k)
                        if g and k == 0:
                            scale_f(b, g - 1)
                        if g == 3 and k == 0 and not last(b):
                            split_x(b + 1)
                        if g and k == 3:
                            gate_f(b, g - 1)
                        if g == 1 and 5 <= k < 5 + TT and not last(b):
                            statistics(b + 1, k - 5)
                    if g + 2 < NG:
                        negate(b, g + 2)
                    if g == 2 and not last(b):
                        newton(b + 1)
                invert_sums(b, 0)
                if not last(b):
                    for c in range(3):
                        chunk_lo(b + 1, c)
                norm_z(b, 0)
                if not last(b):
                    chunk_lo(b + 1, 3)

            for i in range(TT):
                statistics(0, i)
            newton(0)
            dve.wait_ge(hi_done, 1)
            nc.vector.tensor_tensor(wl[:].rearrange("p k n -> p (k n)"), raw_qkv,
                                    wh[:].rearrange("p k n -> p (k n)").bitcast(F32),
                                    ALU.subtract).then_inc(lo_done, 1)
            split_x(0)
            for c in range(4):
                if c == 0:
                    split_gu_lo(0)
                    split_gu_lo(1)
                chunk_lo(0, c)
            dve.wait_ge(hi_done, 4)
            nc.vector.tensor_tensor(wol[:].rearrange("p k n -> p (k n)"), raw_o,
                                    woh[:].rearrange("p k n -> p (k n)").bitcast(F32),
                                    ALU.subtract).then_inc(lo_done, 1)
            dve.wait_ge(hi_done, 5)
            nc.vector.tensor_tensor(wdl[:].rearrange("p m n -> p (m n)"), raw_d,
                                    wdh[:].rearrange("p m n -> p (m n)").bitcast(F32),
                                    ALU.subtract).then_inc(lo_done, 1)
            dve.wait_ge(sc_loaded, 32)
            nc.vector.tensor_scalar(hsg[:], sgt[:, 0, :], 0.5, None, ALU.mult).then_inc(sc_step, 1)
            dve.wait_ge(sc_step, 1)
            nc.vector.tensor_tensor(sgt[:, 2, :], hsg[:], sgt[:, 1, :], ALU.mult).then_inc(sc_step, 1)
            dve.wait_ge(sc_step, 2)
            dve.wait_ge(dve_const, 3)
            batch(0)
            with dve.Fori(1, B - 1) as b:
                batch(b)
            dve.wait_ge(consts, spare)
            batch(B - 1)
            scale_f(B - 1, TT - 1)
            gate_f(B - 1, TT - 1)
            invert_sums(B - 1, 1)
            norm_z(B - 1, 1)
            dve.wait_ge(zhi_done, 2 * B)
            nc.vector.tensor_tensor(zl[:, 1, :], zc, zh[:, 1, :].bitcast(F32), ALU.subtract).then_inc(zlo_done[1], 1)
            dve.wait_ge(x_loaded, 16 * (B + 1))
            for n in range(2):
                finish(B - 1, (n,))
                dve.wait_ge(o_used, 2 * B - 1 + n)
                part = xin[:, 2 * n:2 * n + 2, :]
                nc.vector.tensor_tensor(part, part, u[:, 2 * n:2 * n + 2, :], ALU.add).then_inc(out_done, 1)


def kernel(**inputs):
    import numpy as np
    import concourse.bacc as bacc
    from concourse.bass_utils import run_bass_kernel_spmd as run

    a = {k.replace("L0_", ""): np.asarray(v) for k, v in inputs.items()}
    pad = HIDP - HID
    arrays = {
        "x": a["attn_x"],
        "wqkvT": np.ascontiguousarray(np.concatenate([a["attn_Wq"], a["attn_Wk"], a["attn_Wv"]]).T),
        "woT": np.ascontiguousarray(a["attn_Wo"].T),
        "wgT": np.pad(a["ffn_wq_gate"].T, ((0, 0), (0, pad))),
        "wuT": np.pad(a["ffn_wq_up"].T, ((0, 0), (0, pad))),
        "wdT": np.pad(a["ffn_wq_down"].T, ((0, pad), (0, 0))),
        "sg": np.ascontiguousarray(np.pad(a["ffn_s_gate"], (0, pad)).reshape(HT, P).T),
        "su": np.ascontiguousarray(np.pad(a["ffn_s_up"], (0, pad)).reshape(HT, P).T),
        "sd": a["ffn_s_down"],
    }
    nc = bacc.Bacc("TRN2", target_bir_lowering=False, num_devices=1)
    aps = [nc.dram_tensor(f"in_{n}", v.shape, mybir.dt.from_np(v.dtype), kind="ExternalInput").ap()
           for n, v in arrays.items()]
    out = nc.dram_tensor("out_0", (B, T, D), F32, kind="ExternalOutput").ap()
    build(nc, *aps, out)
    r = run(nc, [{f"in_{n}": v for n, v in arrays.items()}], core_ids=[0])
    return r.results[0]["out_0"]
```
